# Optimizing a Trainium2 kernel written in Bass

```python
import numpy as np
import jax
import jax.numpy as jnp

def _softmax(x, axis=-1):
    return jax.nn.softmax(x, axis=axis)

def _gelu(x):
    return jax.nn.gelu(x, approximate=True)

def _silu(x):
    return jax.nn.silu(x)

def _sigmoid(x):
    return jax.nn.sigmoid(x)

def _layernorm(x, axis=-1, eps=1e-05):
    m = jnp.mean(x, axis=axis, keepdims=True)
    v = jnp.var(x, axis=axis, keepdims=True)
    return (x - m) / jnp.sqrt(v + eps)

def _scatter_add(tgt, idx, src, axis=0):
    return tgt.at[idx].add(src)

def _segment_sum(src, seg, n):
    return jax.ops.segment_sum(src, seg, n)
kernel_name = 'mk_gnn_preln_d4_gnn_r32_636da7'

def setup_inputs(seed: int=0):
    np.random.seed(seed)
    _w = jnp.asarray

    def _rec_inputs():
        import jax
        import jax.numpy as jnp
        _gk = jax.random.key(seed)
        x = -0.0005121 + 1.001 * jax.random.normal(jax.random.fold_in(_gk, 1), (3125, 32), jnp.float32)
        src = jax.random.randint(jax.random.fold_in(_gk, 2), (100000,), 0, 3125, jnp.int32)
        dst = jnp.minimum((3125 * jax.random.uniform(jax.random.fold_in(_gk, 3), (100000,)) ** 2.0).astype(jnp.int32), 99999)
        _o = jnp.argsort(dst, stable=True)
        src = src[_o]
        dst = dst[_o]
        edge_attr_3 = 0.000844983 + 0.999762 * jax.random.normal(jax.random.fold_in(_gk, 12), (100000, 3), jnp.float32)
        edge_attr_32 = 0.000189758 + 1.00013 * jax.random.normal(jax.random.fold_in(_gk, 13), (100000, 32), jnp.float32)
        edge_weight = jax.random.uniform(jax.random.fold_in(_gk, 15), (100000,), jnp.float32, 0.0, 1)
        return (x, src, dst, edge_attr_3, edge_attr_32, edge_weight)
    x, src, dst, edge_attr_3, edge_attr_32, edge_weight = _rec_inputs()

    def _L0_gnn_setup():
        import jax, jax.numpy as jnp
        import numpy as np
        N_NODES = 3125
        N_EDGES = 50000
        NODE_F = 32
        EDGE_F = 32
        HIDDEN = 128
        EPS = 1e-05
        key = jax.random.key(seed)
        ks = jax.random.split(key, 8)
        x = jax.random.normal(ks[0], (N_NODES, NODE_F), dtype=jnp.float32)
        edge_index = jax.random.randint(ks[1], (2, N_EDGES), 0, N_NODES, dtype=jnp.int64)
        edge_attr = jax.random.normal(ks[2], (N_EDGES, EDGE_F), dtype=jnp.float32)
        u = jax.random.normal(ks[3], (1, 8), dtype=jnp.float32)
        batch = jnp.zeros((N_NODES,), dtype=jnp.int64)
        in_f = NODE_F + EDGE_F
        W1 = jax.random.normal(ks[4], (HIDDEN, in_f), dtype=jnp.float32) / np.sqrt(in_f)
        b1 = jnp.zeros((HIDDEN,), dtype=jnp.float32)
        gamma = jnp.ones((HIDDEN,), dtype=jnp.float32)
        beta = jnp.zeros((HIDDEN,), dtype=jnp.float32)
        W2 = jax.random.normal(ks[5], (NODE_F, HIDDEN), dtype=jnp.float32) / np.sqrt(HIDDEN)
        b2 = jnp.zeros((NODE_F,), dtype=jnp.float32)
        return {'x': x, 'edge_index': edge_index, 'edge_attr': edge_attr, 'u': u, 'batch': batch, 'W1': W1, 'b1': b1, 'gamma': gamma, 'beta': beta, 'W2': W2, 'b2': b2}
    _L0_gnn_all = _L0_gnn_setup()
    _L0_gnn_in = {k: v for k, v in _L0_gnn_all.items() if k in ('u', 'W1', 'b1', 'gamma', 'beta', 'W2', 'b2')}
    del _L0_gnn_all

    def _L1_gnn_setup():
        import jax, jax.numpy as jnp
        import numpy as np
        from math import factorial, pi, sqrt
        MUL = 8
        RS = [(MUL, 0), (MUL, 1)]
        N_NODES = 625
        N_EDGES = 20000
        FEAT_DIM = sum((m * (2 * l + 1) for m, l in RS))
        R_DIM = sum((mo * mi * (2 * min(lo, li) + 1) for mo, lo in RS for mi, li in RS))
        HIDDEN = 64

        def _cg(j1, j2, j3, m1, m2, m3):
            if m1 + m2 != m3:
                return 0.0
            f = factorial
            pre = sqrt((2 * j3 + 1) * f(j3 + j1 - j2) * f(j3 - j1 + j2) * f(j1 + j2 - j3) / f(j1 + j2 + j3 + 1))
            pre *= sqrt(f(j3 + m3) * f(j3 - m3) * f(j1 - m1) * f(j1 + m1) * f(j2 - m2) * f(j2 + m2))
            kmin = max(0, j2 - j3 - m1, j1 - j3 + m2)
            kmax = min(j1 + j2 - j3, j1 - m1, j2 + m2)
            s = 0.0
            for k in range(kmin, kmax + 1):
                s += (-1) ** k / (f(k) * f(j1 + j2 - j3 - k) * f(j1 - m1 - k) * f(j2 + m2 - k) * f(j3 - j2 + m1 + k) * f(j3 - j1 - m2 + k))
            return pre * s

        def _w3j_complex(l1, l2, l3):
            w = np.zeros((2 * l1 + 1, 2 * l2 + 1, 2 * l3 + 1))
            for m1 in range(-l1, l1 + 1):
                for m2 in range(-l2, l2 + 1):
                    m3 = -(m1 + m2)
                    if abs(m3) <= l3:
                        w[m1 + l1, m2 + l2, m3 + l3] = (-1) ** (l1 - l2 - m3) / sqrt(2 * l3 + 1) * _cg(l1, l2, l3, m1, m2, -m3)
            return w

        def _A(l):
            A = np.zeros((2 * l + 1, 2 * l + 1), dtype=complex)
            A[l, l] = 1.0
            for m in range(1, l + 1):
                A[l + m, l + m] = (-1) ** m / sqrt(2)
                A[l + m, l - m] = 1.0 / sqrt(2)
                A[l - m, l - m] = 1j / sqrt(2)
                A[l - m, l + m] = -1j * (-1) ** m / sqrt(2)
            return A

        def real_w3j(l1, l2, l3):
            wc = _w3j_complex(l1, l2, l3).astype(complex)
            wr = np.einsum('abc,ma,nb,oc->mno', wc, _A(l1).conj(), _A(l2).conj(), _A(l3).conj())
            i = int(np.argmax(np.abs(wr)))
            ph = wr.flat[i] / abs(wr.flat[i])
            wr = wr / ph
            assert np.abs(wr.imag).max() < 1e-10
            return np.real(wr).astype(np.float32)
        _W3J = {}
        for _mo, _lo in RS:
            for _mi, _li in RS:
                for _lf in range(abs(_lo - _li), _lo + _li + 1):
                    if (_lo, _lf, _li) not in _W3J:
                        _W3J[_lo, _lf, _li] = jnp.asarray(real_w3j(_lo, _lf, _li))
        _NORM = []
        for _mo, _lo in RS:
            _num = sum((mi * (2 * min(_lo, li) + 1) for mi, li in RS))
            _NORM.append(sqrt(4.0 * pi) * sqrt(2.0 * _lo + 1.0) / sqrt(_num))
        _F_OFFS = [0] + list(np.cumsum([mi * (2 * li + 1) for mi, li in RS]))

        def spherical_harmonics(rel_vec):
            r = rel_vec / jnp.linalg.norm(rel_vec, axis=-1, keepdims=True)
            x, y, z = (r[:, 0], r[:, 1], r[:, 2])
            y0 = jnp.full_like(x, 0.5 / sqrt(pi))[:, None]
            c1 = sqrt(3.0 / (4.0 * pi))
            y1 = c1 * jnp.stack([y, z, x], axis=-1)
            c2a = 0.5 * sqrt(15.0 / pi)
            c2b = 0.25 * sqrt(5.0 / pi)
            c2c = 0.25 * sqrt(15.0 / pi)
            y2 = jnp.stack([c2a * x * y, c2a * y * z, c2b * (3.0 * z * z - 1.0), c2a * x * z, c2c * (x * x - y * y)], axis=-1)
            return jnp.concatenate([y0, y1, y2], axis=-1)
        key = jax.random.key(seed)
        ks = jax.random.split(key, 6)
        features = jax.random.normal(ks[0], (N_NODES, FEAT_DIM), dtype=jnp.float32)
        abs_distances = jax.random.uniform(ks[1], (N_EDGES,), dtype=jnp.float32, minval=0.1, maxval=1.0)
        rel_vec = jax.random.normal(ks[2], (N_EDGES, 3), dtype=jnp.float32)
        edge_index = jax.random.randint(ks[3], (2, N_EDGES), 0, N_NODES, dtype=jnp.int32)
        w1 = jax.random.normal(ks[4], (1, HIDDEN), dtype=jnp.float32)
        b1 = jnp.zeros((HIDDEN,), jnp.float32)
        w2 = jax.random.normal(ks[5], (HIDDEN, R_DIM), dtype=jnp.float32) / sqrt(HIDDEN)
        b2 = jnp.zeros((R_DIM,), jnp.float32)
        return {'features': features, 'abs_distances': abs_distances, 'rel_vec': rel_vec, 'edge_index': edge_index, 'w1': w1, 'b1': b1, 'w2': w2, 'b2': b2}
    _L1_gnn_all = _L1_gnn_setup()
    _L1_gnn_in = {k: v for k, v in _L1_gnn_all.items() if k in ('w1', 'b1', 'w2', 'b2')}
    del _L1_gnn_all

    def _L2_gnn_setup():
        import jax, jax.numpy as jnp
        import numpy as np
        NUM_LAYERS = 3
        ALPHA = 0.9
        N_NODES = 3125
        N_CLASSES = 32
        N_EDGES = 100000

        def _gcn_norm(edge_index, edge_weight, num_nodes):
            row, col = (edge_index[0], edge_index[1])
            deg = jax.ops.segment_sum(edge_weight, col, num_segments=num_nodes)
            deg_inv_sqrt = jnp.where(deg > 0, jax.lax.rsqrt(jnp.maximum(deg, 1e-38)), 0.0)
            return deg_inv_sqrt[row] * edge_weight * deg_inv_sqrt[col]
        key = jax.random.key(seed)
        k1, k2, k3 = jax.random.split(key, 3)
        y = jax.random.uniform(k1, (N_NODES, N_CLASSES), dtype=jnp.float32)
        edge_index = jax.random.randint(k2, (2, N_EDGES), 0, N_NODES, dtype=jnp.int64)
        edge_weight = jax.random.uniform(k3, (N_EDGES,), dtype=jnp.float32)
        return {'y': y, 'edge_index': edge_index, 'edge_weight': edge_weight}
    _L2_gnn_all = _L2_gnn_setup()
    _L2_gnn_in = {k: v for k, v in _L2_gnn_all.items() if k in ()}
    del _L2_gnn_all

    def _L3_gnn_setup():
        import jax, jax.numpy as jnp
        import numpy as np
        N_NODES = 3125
        N_EDGES = 50000
        DIM = 32
        N_LAYERS = 3
        BN_EPS = 1e-05

        def _gcn_norm(edge_index, num_nodes):
            src = jnp.concatenate([edge_index[0], jnp.arange(num_nodes, dtype=edge_index.dtype)])
            dst = jnp.concatenate([edge_index[1], jnp.arange(num_nodes, dtype=edge_index.dtype)])
            w = jnp.ones(src.shape[0], dtype=jnp.float32)
            deg = jax.ops.segment_sum(w, dst, num_segments=num_nodes)
            dinv = jnp.where(deg > 0, jax.lax.rsqrt(deg), 0.0)
            wn = dinv[src] * w * dinv[dst]
            return (src, dst, wn)

        def _batchnorm(z, gamma, beta):
            mean = jnp.mean(z, axis=0)
            var = jnp.mean(jnp.square(z - mean), axis=0)
            return (z - mean) * jax.lax.rsqrt(var + BN_EPS) * gamma + beta
        key = jax.random.key(seed)
        k1, k2 = jax.random.split(key)
        x = jax.random.normal(k1, (N_NODES, DIM), dtype=jnp.float32)
        edge_index = jax.random.randint(k2, (2, N_EDGES), 0, N_NODES, dtype=jnp.int32)
        src, dst = (edge_index[0], edge_index[1])
        dst = jnp.where(src == dst, (dst + 1) % N_NODES, dst)
        edge_index = jnp.stack([src, dst])
        gammas = jnp.ones((N_LAYERS, DIM), dtype=jnp.float32)
        betas = jnp.zeros((N_LAYERS, DIM), dtype=jnp.float32)
        return {'x': x, 'edge_index': edge_index, 'gammas': gammas, 'betas': betas}
    _L3_gnn_all = _L3_gnn_setup()
    _L3_gnn_in = {k: v for k, v in _L3_gnn_all.items() if k in ('gammas', 'betas')}
    del _L3_gnn_all
    return {'x': x, 'src': src, 'dst': dst, 'edge_attr_3': edge_attr_3, 'edge_attr_32': edge_attr_32, 'edge_weight': edge_weight, 'L0_gnn_u': _L0_gnn_in['u'], 'L0_gnn_W1': _L0_gnn_in['W1'], 'L0_gnn_b1': _L0_gnn_in['b1'], 'L0_gnn_gamma': _L0_gnn_in['gamma'], 'L0_gnn_beta': _L0_gnn_in['beta'], 'L0_gnn_W2': _L0_gnn_in['W2'], 'L0_gnn_b2': _L0_gnn_in['b2'], 'L1_gnn_w1': _L1_gnn_in['w1'], 'L1_gnn_b1': _L1_gnn_in['b1'], 'L1_gnn_w2': _L1_gnn_in['w2'], 'L1_gnn_b2': _L1_gnn_in['b2'], 'L3_gnn_gammas': _L3_gnn_in['gammas'], 'L3_gnn_betas': _L3_gnn_in['betas']}

def reference(x, src, dst, edge_attr_3, edge_attr_32, edge_weight, L0_gnn_u, L0_gnn_W1, L0_gnn_b1, L0_gnn_gamma, L0_gnn_beta, L0_gnn_W2, L0_gnn_b2, L1_gnn_w1, L1_gnn_b1, L1_gnn_w2, L1_gnn_b2, L3_gnn_gammas, L3_gnn_betas):
    import jax
    import jax.numpy as jnp

    def _L0_gnn_ref(x, edge_index, edge_attr, u, batch, W1, b1, gamma, beta, W2, b2):
        import jax, jax.numpy as jnp
        import numpy as np
        N_NODES = 3125
        N_EDGES = 50000
        NODE_F = 32
        EDGE_F = 32
        HIDDEN = 128
        EPS = 1e-05
        row = edge_index[0]
        agg = jax.ops.segment_sum(edge_attr, row, num_segments=x.shape[0])
        out = jnp.concatenate([x, agg], axis=1)
        h = out @ W1.T + b1
        h = jax.nn.relu(h)
        mean = jnp.mean(h, axis=0)
        var = jnp.var(h, axis=0)
        h = (h - mean) * jax.lax.rsqrt(var + EPS) * gamma + beta
        return h @ W2.T + b2

    def _L1_gnn_ref(features, abs_distances, rel_vec, edge_index, w1, b1, w2, b2):
        import jax, jax.numpy as jnp
        import numpy as np
        from math import factorial, pi, sqrt
        MUL = 8
        RS = [(MUL, 0), (MUL, 1)]
        N_NODES = 625
        N_EDGES = 20000
        FEAT_DIM = sum((m * (2 * l + 1) for m, l in RS))
        R_DIM = sum((mo * mi * (2 * min(lo, li) + 1) for mo, lo in RS for mi, li in RS))
        HIDDEN = 64

        def _cg(j1, j2, j3, m1, m2, m3):
            if m1 + m2 != m3:
                return 0.0
            f = factorial
            pre = sqrt((2 * j3 + 1) * f(j3 + j1 - j2) * f(j3 - j1 + j2) * f(j1 + j2 - j3) / f(j1 + j2 + j3 + 1))
            pre *= sqrt(f(j3 + m3) * f(j3 - m3) * f(j1 - m1) * f(j1 + m1) * f(j2 - m2) * f(j2 + m2))
            kmin = max(0, j2 - j3 - m1, j1 - j3 + m2)
            kmax = min(j1 + j2 - j3, j1 - m1, j2 + m2)
            s = 0.0
            for k in range(kmin, kmax + 1):
                s += (-1) ** k / (f(k) * f(j1 + j2 - j3 - k) * f(j1 - m1 - k) * f(j2 + m2 - k) * f(j3 - j2 + m1 + k) * f(j3 - j1 - m2 + k))
            return pre * s

        def _w3j_complex(l1, l2, l3):
            w = np.zeros((2 * l1 + 1, 2 * l2 + 1, 2 * l3 + 1))
            for m1 in range(-l1, l1 + 1):
                for m2 in range(-l2, l2 + 1):
                    m3 = -(m1 + m2)
                    if abs(m3) <= l3:
                        w[m1 + l1, m2 + l2, m3 + l3] = (-1) ** (l1 - l2 - m3) / sqrt(2 * l3 + 1) * _cg(l1, l2, l3, m1, m2, -m3)
            return w

        def _A(l):
            A = np.zeros((2 * l + 1, 2 * l + 1), dtype=complex)
            A[l, l] = 1.0
            for m in range(1, l + 1):
                A[l + m, l + m] = (-1) ** m / sqrt(2)
                A[l + m, l - m] = 1.0 / sqrt(2)
                A[l - m, l - m] = 1j / sqrt(2)
                A[l - m, l + m] = -1j * (-1) ** m / sqrt(2)
            return A

        def real_w3j(l1, l2, l3):
            wc = _w3j_complex(l1, l2, l3).astype(complex)
            wr = np.einsum('abc,ma,nb,oc->mno', wc, _A(l1).conj(), _A(l2).conj(), _A(l3).conj())
            i = int(np.argmax(np.abs(wr)))
            ph = wr.flat[i] / abs(wr.flat[i])
            wr = wr / ph
            assert np.abs(wr.imag).max() < 1e-10
            return np.real(wr).astype(np.float32)
        _W3J = {}
        for _mo, _lo in RS:
            for _mi, _li in RS:
                for _lf in range(abs(_lo - _li), _lo + _li + 1):
                    if (_lo, _lf, _li) not in _W3J:
                        _W3J[_lo, _lf, _li] = jnp.asarray(real_w3j(_lo, _lf, _li))
        _NORM = []
        for _mo, _lo in RS:
            _num = sum((mi * (2 * min(_lo, li) + 1) for mi, li in RS))
            _NORM.append(sqrt(4.0 * pi) * sqrt(2.0 * _lo + 1.0) / sqrt(_num))
        _F_OFFS = [0] + list(np.cumsum([mi * (2 * li + 1) for mi, li in RS]))

        def spherical_harmonics(rel_vec):
            r = rel_vec / jnp.linalg.norm(rel_vec, axis=-1, keepdims=True)
            x, y, z = (r[:, 0], r[:, 1], r[:, 2])
            y0 = jnp.full_like(x, 0.5 / sqrt(pi))[:, None]
            c1 = sqrt(3.0 / (4.0 * pi))
            y1 = c1 * jnp.stack([y, z, x], axis=-1)
            c2a = 0.5 * sqrt(15.0 / pi)
            c2b = 0.25 * sqrt(5.0 / pi)
            c2c = 0.25 * sqrt(15.0 / pi)
            y2 = jnp.stack([c2a * x * y, c2a * y * z, c2b * (3.0 * z * z - 1.0), c2a * x * z, c2c * (x * x - y * y)], axis=-1)
            return jnp.concatenate([y0, y1, y2], axis=-1)
        src, dst = (edge_index[0], edge_index[1])
        R = jax.nn.relu(abs_distances[:, None] @ w1 + b1) @ w2 + b2
        Y = spherical_harmonics(rel_vec)
        Fj = features[src]
        E = Fj.shape[0]
        msg_blocks = []
        r_off = 0
        for i, (mo, lo) in enumerate(RS):
            acc = jnp.zeros((E, mo, 2 * lo + 1), dtype=features.dtype)
            for j, (mi, li) in enumerate(RS):
                n_lf = 2 * min(lo, li) + 1
                sz = mo * mi * n_lf
                Rb = R[:, r_off:r_off + sz].reshape(E, mo, mi, n_lf)
                r_off += sz
                Fb = Fj[:, _F_OFFS[j]:_F_OFFS[j + 1]].reshape(E, mi, 2 * li + 1)
                for k, lf in enumerate(range(abs(lo - li), lo + li + 1)):
                    C = _W3J[lo, lf, li]
                    Yf = Y[:, lf * lf:(lf + 1) * (lf + 1)]
                    acc = acc + _NORM[i] * jnp.einsum('euv,ef,evi,ofi->euo', Rb[..., k], Yf, Fb, C)
            msg_blocks.append(acc.reshape(E, -1))
        msg = jnp.concatenate(msg_blocks, axis=-1)
        out = jnp.zeros((features.shape[0], msg.shape[1]), dtype=features.dtype)
        out = out.at[dst].add(msg)
        return out

    def _L2_gnn_ref(y, edge_index, edge_weight):
        import jax, jax.numpy as jnp
        import numpy as np
        NUM_LAYERS = 3
        ALPHA = 0.9
        N_NODES = 3125
        N_CLASSES = 32
        N_EDGES = 100000

        def _gcn_norm(edge_index, edge_weight, num_nodes):
            row, col = (edge_index[0], edge_index[1])
            deg = jax.ops.segment_sum(edge_weight, col, num_segments=num_nodes)
            deg_inv_sqrt = jnp.where(deg > 0, jax.lax.rsqrt(jnp.maximum(deg, 1e-38)), 0.0)
            return deg_inv_sqrt[row] * edge_weight * deg_inv_sqrt[col]
        num_nodes = y.shape[0]
        row, col = (edge_index[0], edge_index[1])
        norm = _gcn_norm(edge_index, edge_weight, num_nodes)
        res = (1.0 - ALPHA) * y
        out = y
        for _ in range(NUM_LAYERS):
            msg = norm[:, None] * out[row]
            agg = jax.ops.segment_sum(msg, col, num_segments=num_nodes)
            out = jnp.clip(agg * ALPHA + res, 0.0, 1.0)
        return out

    def _L3_gnn_ref(x, edge_index, gammas, betas):
        import jax, jax.numpy as jnp
        import numpy as np
        N_NODES = 3125
        N_EDGES = 50000
        DIM = 32
        N_LAYERS = 3
        BN_EPS = 1e-05

        def _gcn_norm(edge_index, num_nodes):
            src = jnp.concatenate([edge_index[0], jnp.arange(num_nodes, dtype=edge_index.dtype)])
            dst = jnp.concatenate([edge_index[1], jnp.arange(num_nodes, dtype=edge_index.dtype)])
            w = jnp.ones(src.shape[0], dtype=jnp.float32)
            deg = jax.ops.segment_sum(w, dst, num_segments=num_nodes)
            dinv = jnp.where(deg > 0, jax.lax.rsqrt(deg), 0.0)
            wn = dinv[src] * w * dinv[dst]
            return (src, dst, wn)

        def _batchnorm(z, gamma, beta):
            mean = jnp.mean(z, axis=0)
            var = jnp.mean(jnp.square(z - mean), axis=0)
            return (z - mean) * jax.lax.rsqrt(var + BN_EPS) * gamma + beta
        n = x.shape[0]
        src, dst, wn = _gcn_norm(edge_index, n)
        z = x
        for i in range(N_LAYERS):
            msg = wn[:, None] * z[src]
            z = jax.ops.segment_sum(msg, dst, num_segments=n)
            z = jax.nn.relu(z)
            z = _batchnorm(z, gammas[i], betas[i])
        return z
    edge_index = jnp.stack([src, dst])
    batch0 = jnp.zeros((3125,), jnp.int32)
    h = jnp.maximum(_layernorm(x, axis=-1), 0.0)
    x = x + _L0_gnn_ref(h, edge_index, edge_attr_32, L0_gnn_u, batch0, L0_gnn_W1, L0_gnn_b1, L0_gnn_gamma, L0_gnn_beta, L0_gnn_W2, L0_gnn_b2)
    h = jnp.maximum(_layernorm(x, axis=-1), 0.0)
    x = x + _L1_gnn_ref(h, edge_weight, edge_attr_3, edge_index, L1_gnn_w1, L1_gnn_b1, L1_gnn_w2, L1_gnn_b2)
    h = jnp.maximum(_layernorm(x, axis=-1), 0.0)
    x = x + _L2_gnn_ref(h, edge_index, edge_weight)
    h = jnp.maximum(_layernorm(x, axis=-1), 0.0)
    x = x + _L3_gnn_ref(h, edge_index, L3_gnn_gammas, L3_gnn_betas)
    return x

_drawn_inputs = setup_inputs


def setup_inputs(seed=0):
    import zlib

    import numpy as np

    out = dict(_drawn_inputs(seed))
    spreads = {'L0_gnn_b1': (0.0, 0.8),
     'L0_gnn_gamma': (1.0, 0.2),
     'L0_gnn_beta': (0.0, 0.1),
     'L0_gnn_b2': (0.0, 0.1),
     'L1_gnn_b1': (0.0, 0.1),
     'L1_gnn_b2': (0.0, 0.1),
     'L3_gnn_gammas': (1.0, 0.2),
     'L3_gnn_betas': (0.0, 0.1)}
    factors = {}
    for name, (base, spread) in spreads.items():
        noise = np.random.default_rng([zlib.crc32(name.encode()), seed]).standard_normal(out[name].shape)
        drawn = base * np.exp(spread * noise) if base else spread * noise
        out[name] = jnp.asarray(drawn.astype(out[name].dtype))
    for name, factor in factors.items():
        out[name] = (out[name] * factor).astype(out[name].dtype)
    return out
```

```python
from contextlib import ExitStack
from math import sqrt

import concourse.bass as bass
from concourse import mybir

ALU = mybir.AluOpType
ACT = mybir.ActivationFunctionType
F32 = mybir.dt.float32
BF16 = mybir.dt.bfloat16
I32 = mybir.dt.int32
AX = mybir.AxisListType.X

P = 128
NODES, EDGES, FEAT = 3125, 100000, 32
NA = -(-NODES // P)
NP = NA * P
LAST = NODES - (NA - 1) * P
CH = 784
STEPS = CH // 4
PAIRS = CH // 2
NA2 = -(-NODES // (2 * P))
A_LO = 13
HID0, HID1 = 128, 64
MSG = 34
ROW = 96
NCOL = [(n, min(512, NP - n)) for n in range(0, NP, 512)]
EPS = 1e-5
ALPHA = 0.9
BIG = NP * NP


def ds(start, size):
    if isinstance(start, int):
        return slice(start, start + size)
    return bass.ds(start, size)


def gnn_program(nc, x_in, src_in, dst_in, srcT_in, dstT_in, ea3_in, ea32_in, ew_in, ewT_in,
                w1T_in, b1_in, gamma_in, beta_in, w2T_in, b2_in, l1w1_in, l1b1_in, l1w2_in, l1b2_in,
                gam3_in, bet3_in, out):
    with ExitStack() as ctx:
        def sb(name, shape, dt=F32):
            return ctx.enter_context(nc.sbuf_tensor(name, shape, dt))

        def sem(name):
            return ctx.enter_context(nc.semaphore(name))

        adj_w = nc.dram_tensor("adj_w", [BIG + 2 * P, 1], F32, kind="Internal").ap()
        adj_c = nc.dram_tensor("adj_c", [BIG + 2 * P, 1], F32, kind="Internal").ap()
        keys_dram = nc.dram_tensor("keys_dram", [CH, P], F32, kind="Internal").ap()
        feat_dram = nc.dram_tensor("feat_dram", [NP, ROW], F32, kind="Internal").ap()

        ident = sb("ident", [P, P])
        stack_id = sb("stack_id", [P, 32])
        iota_b = sb("iota_b", [P, 2 * P])
        iota_a = sb("iota_a", [P, NA2])
        earlier = sb("earlier", [P, P], BF16)
        spare = sb("spare", [P, 2])
        ones_bf = sb("ones_bf", [P, 1], BF16)
        ones_f = sb("ones_f", [P, P])
        zero_bf = sb("zero_bf", [P, 512], BF16)
        valid = sb("valid", [P, NA])

        src_i = sb("src_i", [P, CH], I32)
        dst_i = sb("dst_i", [P, CH], I32)
        key = sb("key", [P, CH])
        to_spare = sb("to_spare", [P, CH])
        a_src = sb("a_src", [P, CH])
        b_src = sb("b_src", [P, CH])
        a_dst = sb("a_dst", [P, CH])
        b_dst = sb("b_dst", [P, CH])
        wt = sb("wt", [P, CH])
        wparts = sb("wparts", [P, CH, 7], BF16)
        rlen = sb("rlen", [P, CH])
        rinv = sb("rinv", [P, CH])
        rdir = sb("rdir", [P, CH, 5])
        sc_idx = sb("sc_idx", [P, CH])
        sc_val = sb("sc_val", [P, PAIRS, 2, 2])
        add_to = sb("add_to", [P, 2, 2], I32)
        add_val = sb("add_val", [P, 2, 2, 2])
        pause = sb("pause", [1, 3])
        take_from = sb("take_from", [P, 2, 4], I32)

        keyrow = sb("keyrow", [P, 2, 2 * P])
        key_gap = sb("key_gap", [P, 2, 2 * P])
        same = sb("same", [P, 2, 2, 2 * P], BF16)
        same_tri = sb("same_tri", [P, 2, 2, P], BF16)
        offs = sb("offs", [P, 2])
        attr = sb("attr", [P, 2, 4, FEAT])
        dist2 = sb("dist2", [P, 4, 2 * P])
        onehot = sb("onehot", [P, 2, 4, 2 * P])
        prod = sb("prod", [P, 2, 4, NA2 * MSG + 6])
        wrow = sb("wrow", [HID1, 2, 4 * P])
        hidT = sb("hidT", [HID1 + 1, 2, 4 * P])
        gath = sb("gath", [P, 2, 4, ROW])
        cross1 = sb("cross1", [P, 4, 3, 8])
        cross2 = sb("cross2", [P, 4, 3, 8])
        dots = sb("dots", [P, 4, 8, 3])
        terms = sb("terms", [P, 2, 2, 40 * 16])
        res = sb("res", [P, 2, 4, 42])
        along = sb("along", [P, 4, 8, 3])

        w1T = sb("w1T", [64, HID0])
        b1 = sb("b1", [HID0, 1])
        gamma = sb("gamma", [HID0, 1])
        beta = sb("beta", [HID0, 1])
        w2T = sb("w2T", [HID0, FEAT])
        b2b = sb("b2b", [P, FEAT])
        l1w1 = sb("l1w1", [HID1, 1])
        l1b1 = sb("l1b1", [HID1, 1])
        w2raw = sb("w2raw", [HID1 + 1, 384])
        w2mix = sb("w2mix", [HID1 + 1, 384])
        gam3 = sb("gam3", [P, 3, FEAT])
        bet3 = sb("bet3", [P, 3, FEAT])

        x = sb("x", [P, NA, FEAT])
        h = sb("h", [P, NA, FEAT])
        zn = sb("zn", [P, NA, FEAT])
        cen = sb("cen", [P, NA, FEAT])
        sq = sb("sq", [P, NA, FEAT])
        st = sb("st", [P, 4, NA])
        deg = sb("deg", [P, NA, 2])
        dinv = sb("dinv", [P, 2, NA])
        fsum = sb("fsum", [P, 6, FEAT])
        bnst = sb("bnst", [P, len(NCOL), 6])
        bnagg = sb("bnagg", [P, 6])
        zring = sb("zring", [P, 8, FEAT])

        big = sb("big", [P, 4, NP])
        zeros = big[:, 0, :]
        table = big[:, 0, 0:NA * ROW].rearrange("p (a r) -> p a r", a=NA)
        cat = big[:, 1, 0:NA * 64].rearrange("p (a r) -> p a r", a=NA)
        catT = big[0:64, 2, :]
        actT = big[:, 3, :]
        rel = big[:, 1, 0:CH * 3].rearrange("p (c i) -> p c i", i=3)
        rel2 = big[:, 2, 0:CH * 3].rearrange("p (c i) -> p c i", i=3)
        tmp_i = big[:, 3, 0:CH].bitcast(I32)
        wrest = big[:, 3, CH:2 * CH]
        prod_all = prod[:, :, :, :].rearrange("p q k n -> p (q k n)")
        srcT = prod_all[0:112, 0:7 * P].bitcast(I32)
        dstT = prod_all[0:112, 7 * P:14 * P].bitcast(I32)
        keyT = prod_all[0:112, 14 * P:21 * P]
        normT = big[:, 1, :]
        aggT = prod_all[:, 0:NP]

        ps = ctx.enter_context(nc.psum_tensor("ps", [P, 8, 512], F32))

        s_in = {n: sem("in_" + n) for n in ("idx", "idxT", "rel", "w", "x", "wts")}
        s_const = sem("const")
        s_zero = sem("zeros_set")
        s_zeroed = sem("adj_zeroed")
        s_keyT = sem("keyT_ready")
        s_keysd = sem("keys_in_dram")
        s_dve = sem("dve_chain")
        s_edge = sem("edge_data_ready")
        s_rlen2 = sem("rel_sq_ready")
        s_rlen = sem("rel_len_ready")
        s_krow = [sem(f"keyrow{q}") for q in range(2)]
        s_attr = [sem(f"attr{q}") for q in range(2)]
        s_wrow = [sem(f"wrow{q}") for q in range(2)]
        s_gath = [sem(f"gath{q}") for q in range(2)]
        s_gap = sem("key_gap_ready")
        s_same = sem("same_ready")
        s_tri = sem("same_tri_ready")
        s_ded = sem("merged_ready")
        s_offs = sem("offs_ready")
        s_idx = sem("scatter_rows_ready")
        s_addto = sem("add_rows_placed")
        s_addval = sem("add_values_placed")
        s_take = sem("gather_rows_placed")
        s_aw = sem("adj_w_added")
        s_ac = sem("adj_c_added")
        s_dist = [sem(f"p{n}_dist_ready") for n in range(2)]
        s_oh = [sem(f"p{n}_onehot_ready") for n in range(2)]
        s_prod = [sem(f"p{n}_prod_ready") for n in range(2)]
        s_sum = [sem(f"p{n}_chunk_summed") for n in range(2)]
        s_open = sem("acc_open")
        s_hid = sem("hidden_ready")
        s_rad = sem("radial_ready")
        s_radfree = sem("radial_used")
        s_cross = sem("cross_terms_ready")
        s_vec = sem("vectors_ready")
        s_terms = sem("terms_ready")
        s_red = sem("terms_summed")
        s_along = sem("along_ready")
        s_msg = sem("messages_ready")
        s_wcol = sem("weight_column_ready")
        s_var = sem("var_ready")
        s_std = sem("std_ready")
        s_cat = sem("cat_ready")
        s_catT = sem("catT_in_psum")
        s_catTc = sem("catT_copied")
        s_h0 = sem("hidden0_in_psum")
        s_act0 = sem("act0_ready")
        s_norm = sem("norm0_ready")
        s_out0 = sem("out0_in_psum")
        s_w2 = sem("w2mix_ready")
        s_table = sem("table_ready")
        s_feat = sem("feat_in_dram")
        s_z = sem("z_ready")
        s_zr = sem("zring_ready")
        s_blk = [sem(f"adj_block{q}") for q in range(4)]
        s_mm = sem("block_used")
        s_aggc = sem("agg_copied")
        s_agga = sem("agg_copied_act")
        s_turn = sem("agg_turned")
        s_fs = sem("feature_sums")
        s_fsp = sem("feature_sums_in_psum")
        s_fin = sem("result_ready")
        s_out = sem("out_stored")

        def steps(eng, body):
            for s in range(2):
                body(s, s, 0)
            with eng.Fori(1, STEPS // 2 - 1) as t:
                for q in range(2):
                    body(t * 2 + q, q, t)
            for s in range(STEPS - 2, STEPS):
                body(s, s % 2, s // 2)

        def first(s, n=2):
            return isinstance(s, int) and s < n

        def after(s, n=1):
            return isinstance(s, int) and s >= STEPS - n

        block = ctx.enter_context(nc.Block())

        @block.sync
        def _(sp):
            sp.dma_start(srcT, srcT_in).then_inc(s_in["idxT"], 16)
            sp.dma_start(dstT, dstT_in).then_inc(s_in["idxT"], 16)
            sp.dma_start(src_i[:, :], src_in).then_inc(s_in["idx"], 16)
            sp.dma_start(dst_i[:, :], dst_in).then_inc(s_in["idx"], 16)
            sp.dma_start(wt[:, :], ew_in).then_inc(s_in["w"], 16)
            sp.dma_start(x[:, :, :], x_in.rearrange("(a b) f -> b a f", b=P)).then_inc(s_in["x"], 16)
            sp.dma_start(rel[:, :, :], ea3_in).then_inc(s_in["rel"], 16)
            loads = [(w1T[:, :], w1T_in), (b1[:, :], b1_in), (gamma[:, :], gamma_in), (beta[:, :], beta_in),
                     (w2T[:, :], w2T_in), (b2b[:, :], b2_in.broadcast_to([P, FEAT])),
                     (l1w1[:, :], l1w1_in), (l1b1[:, :], l1b1_in),
                     (w2raw[0:HID1, :], l1w2_in), (w2raw[HID1:HID1 + 1, :], l1b2_in),
                     (gam3[:, :, :], gam3_in.broadcast_to([P, 3 * FEAT]).rearrange("p (l f) -> p l f", l=3)),
                     (bet3[:, :, :], bet3_in.broadcast_to([P, 3 * FEAT]).rearrange("p (l f) -> p l f", l=3))]
            for dst, src in loads:
                sp.dma_start(dst, src).then_inc(s_in["wts"], 16)

            sp.wait_ge(s_keyT, 1)
            sp.dma_start(keys_dram.rearrange("(q j) p -> q (j p)", j=7), keyT).then_inc(s_keysd, 16)
            sp.wait_ge(s_keysd, 16)

            def load_keys(d, q):
                if not first(d):
                    sp.wait_ge(s_gap, 2 * (d - 1))
                row = keys_dram[ds(2 * d, 2), :].rearrange("(o c) p -> o (c p)", o=1)
                sp.dma_start(keyrow[:, q, :], row.broadcast_to([P, 2 * P])).then_inc(s_krow[q], 16)

            def load0(s, q, t):
                load_keys(s, q)
                if not first(s):
                    sp.wait_ge(s_prod[0], 4 * (s - 1))
                sp.dma_start(attr[:, q, :, :].rearrange("p k f -> p (k f)"),
                             ea32_in[:, ds(s * (4 * FEAT), 4 * FEAT)]).then_inc(s_attr[q], 16)

            steps(sp, load0)
            sp.wait_ge(s_table, 1)
            sp.dma_start(feat_dram.rearrange("(a b) r -> b a r", b=P), table).then_inc(s_feat, 16)

            def load1(s, q, t):
                load_keys(s + STEPS, q)
                if not first(s):
                    sp.wait_ge(s_hid, s - 1)
                row = ewT_in[ds(4 * s, 4), :].rearrange("(o c) p -> o (c p)", o=1)
                sp.dma_start(wrow[:, q, :], row.broadcast_to([HID1, 4 * P])).then_inc(s_wrow[q], 16)

            steps(sp, load1)

            sp.wait_ge(s_aw, 32 * PAIRS)
            for r in range(6):
                adj = (adj_w if r < 3 else adj_c)[0:BIG, :].rearrange("(s d) o -> s (d o)", d=NP)
                if r == 3:
                    sp.wait_ge(s_ac, 32 * PAIRS)
                if r == 0:
                    sp.wait_ge(s_feat, 16)

                def load_block(m, slot, used):
                    if used > 0 if isinstance(used, int) else True:
                        sp.wait_ge(s_mm, used)
                    sp.dma_start(big[:, slot, :], adj[ds(m * P, P), :]).then_inc(s_blk[slot], 16)

                for m in range(8):
                    used = NA * r + m - 3 if m >= 4 else NA * r + (m - 4 if m else 0)
                    load_block(m, m % 4, used)
                with sp.Fori(1, NA // 8) as i:
                    for j in range(8):
                        load_block(i * 8 + j, j % 4, i * 8 + (NA * r + j - 3))
                load_block(NA - 1, 0, NA * r + NA - 4)

            sp.wait_ge(s_fin, 1)
            sp.dma_start(out[0:(NA - 1) * P, :].rearrange("(a b) f -> b a f", b=P),
                         x[:, 0:NA - 1, :]).then_inc(s_out, 16)
            sp.dma_start(out[(NA - 1) * P:NODES, :], x[0:LAST, NA - 1, :]).then_inc(s_out, 16)
            sp.wait_ge(s_out, 32)

        @block.gpsimd
        def _(pool):
            pool.memset(zeros, 0.0).then_inc(s_zero, 1)
            pool.memset(ident[:, :], 0.0).then_inc(s_const, 1)
            pool.memset(earlier[:, :], 1.0).then_inc(s_const, 1)
            pool.memset(valid[:, :], 1.0).then_inc(s_const, 1)
            pool.wait_ge(s_const, 3)
            pool.affine_select(out=ident[:, :], in_=ident[:, :], compare_op=ALU.not_equal, fill=1.0,
                               base=0, pattern=[[-1, P]], channel_multiplier=1).then_inc(s_const, 1)
            pool.affine_select(out=earlier[:, :], in_=earlier[:, :], compare_op=ALU.is_gt, fill=0.0,
                               base=0, pattern=[[1, P]], channel_multiplier=-1).then_inc(s_const, 1)
            pool.affine_select(out=valid[:, :], in_=valid[:, :], compare_op=ALU.is_gt, fill=0.0,
                               base=NODES, pattern=[[-P, NA]], channel_multiplier=-1).then_inc(s_const, 1)
            pool.iota(iota_b[:, :], [[1, 2 * P]], base=0, channel_multiplier=0,
                      allow_small_or_imprecise_dtypes=True).then_inc(s_const, 1)
            pool.iota(iota_a[:, :], [[1, NA2]], base=0, channel_multiplier=0,
                      allow_small_or_imprecise_dtypes=True).then_inc(s_const, 1)
            pool.iota(spare[:, :], [[P, 2]], base=BIG, channel_multiplier=1,
                      allow_small_or_imprecise_dtypes=True).then_inc(s_const, 1)

            last_entry = pool.to_reg(BIG + 2 * P - 1)
            last_node = pool.to_reg(NP - 1)

            def snap(v):
                return v if isinstance(v, int) else pool.snap(v)

            def hold_for_waits(n):
                pool.tensor_tensor(pause[:, n:n + 1], spare[0:1, 0:1], spare[0:1, 1:2], ALU.add)

            def add_pair(d, q):
                ready, landed = snap(d + 1), snap(d * 32)
                idx, val = sc_idx[:, ds(2 * d, 2)], sc_val[:, ds(d, 1), :, :].rearrange("p d v j -> p (d v) j")
                pool.wait_ge(s_idx, ready)
                pool.tensor_copy(add_to[:, q, :], idx).then_inc(s_addto, 1)
                pool.tensor_copy(add_val[:, q, :, :], val).then_inc(s_addval, 1)
                pool.wait_ge(s_addto, ready)
                pool.wait_ge(s_addval, ready)
                for v, (adj, done) in enumerate(((adj_c, s_ac), (adj_w, s_aw))):
                    if not first(d, 1):
                        pool.wait_ge(done, landed)
                    hold_for_waits(v)
                    for j in range(2):
                        pool.indirect_dma_start(adj, bass.IndirectOffsetOnAxis(ap=add_to[:, q, j:j + 1], axis=0),
                                                add_val[:, q, v, j:j + 1], None, bounds_check=last_entry,
                                                compute_op=ALU.add).then_inc(done, 16)

            pool.wait_ge(s_zeroed, 16 * 52)

            def phase0(s, q, t):
                add_pair(s, q)

            steps(pool, phase0)
            pool.wait_ge(s_feat, 16)

            def gather(s, q):
                used, taken, rows = snap(2 * (s - 1)) if not first(s) else 0, snap(s + 1), src_i[:, ds(4 * s, 4)]
                if not first(s):
                    pool.wait_ge(s_terms, used)
                pool.tensor_copy(take_from[:, q, :], rows).then_inc(s_take, 1)
                pool.wait_ge(s_take, taken)
                hold_for_waits(2)
                for k in range(4):
                    pool.indirect_dma_start(gath[:, q, k, :], None, feat_dram,
                                            bass.IndirectOffsetOnAxis(ap=take_from[:, q, k:k + 1], axis=0),
                                            bounds_check=last_node).then_inc(s_gath[q], 16)

            gather(0, 0)

            def phase1(s, q, t):
                if not after(s):
                    gather(s + 1, 1 - q)
                add_pair(s + STEPS, q)

            steps(pool, phase1)

        @block.scalar
        def _(act):
            act.wait_ge(s_zero, 1)
            for adj in (adj_w, adj_c):
                act.dma_start(adj[BIG:BIG + 2 * P, :].rearrange("(p c) o -> p (c o)", p=P),
                              zeros[:, 0:2]).then_inc(s_zeroed, 16)

            def zero_block(a, adj):
                act.dma_start(adj[ds(a * (P * NP), P * NP), :].rearrange("(p c) o -> p (c o)", p=P),
                              zeros).then_inc(s_zeroed, 16)

            ln = [0]

            def std():
                ln[0] += 1
                act.wait_ge(s_var, ln[0])
                act.activation(st[:, 3, :], st[:, 2, :], ACT.Sqrt).then_inc(s_std, 1)

            std()
            act.wait_ge(s_rlen2, 1)
            act.activation(rlen[:, :], rinv[:, :], ACT.Sqrt).then_inc(s_rlen, 1)
            act.wait_ge(s_const, 9)

            def compare(d, q):
                act.wait_ge(s_krow[q], d * 8 - q * 8 + 16)
                if not first(d, 1):
                    act.wait_ge(s_same, d)
                for i in range(2):
                    act.activation(key_gap[:, i, :], keyrow[:, q, :], ACT.Square, scale=-1.0,
                                   bias=key[:, ds(2 * d + i, 1)]).then_inc(s_gap, 1)
                act.wait_ge(s_gap, 2 * d + 2)
                if not first(d):
                    act.wait_ge(s_ded, d - 1)
                act.activation(same[:, q, :, :], key_gap[:, :, :], ACT.Relu, scale=-1.0,
                               bias=1.0).then_inc(s_same, 1)

            def onehots(n, s, q, bcol):
                if not first(s, 1):
                    act.wait_ge(s_oh[n], s)
                for k in range(4):
                    act.activation(dist2[:, k, :], iota_b[:, :], ACT.Square, scale=-1.0,
                                   bias=bcol[:, ds(4 * s + k, 1)]).then_inc(s_dist[n], 1)
                act.wait_ge(s_dist[n], 4 * (s + 1))
                if not first(s):
                    act.wait_ge(s_sum[n], 4 * (s - 1))
                act.activation(onehot[:, q, :, :], dist2[:, :, :], ACT.Relu, scale=-1.0,
                               bias=1.0).then_inc(s_oh[n], 1)

            act.wait_ge(s_edge, 1)

            def phase0(s, q, t):
                compare(s, q)
                onehots(0, s, q, b_src)

            def phase0_and_zeros(s, q, t):
                zero_block(t, (adj_w, adj_c)[q])
                phase0(s, q, t)

            for q in range(2):
                phase0_and_zeros(q, q, 0)
            with act.Fori(1, NA) as t:
                for q in range(2):
                    phase0_and_zeros(t * 2 + q, q, t)
            with act.Fori(NA, STEPS // 2) as t:
                for q in range(2):
                    phase0(t * 2 + q, q, t)

            for n, (c0, w) in enumerate(NCOL):
                act.wait_ge(s_h0, n + 1)
                act.activation(actT[:, c0:c0 + w], ps[:, 6 + n % 2, 0:w], ACT.Relu,
                               bias=b1[:, 0:1]).then_inc(s_act0, 1)
            act.wait_ge(s_var, 2)
            act.activation(bnagg[:, 3:4], bnagg[:, 2:3], ACT.Sqrt).then_inc(s_std, 1)
            ln[0] += 1
            std()

            def phase1(s, q, t):
                compare(s + STEPS, q)
                act.wait_ge(s_wrow[q], 16 * (t + 1))
                if not first(s):
                    act.wait_ge(s_rad, 2 * (s - 1))
                act.activation(hidT[0:HID1, q, :], wrow[:, q, :], ACT.Relu, scale=l1w1[:, 0:1],
                               bias=l1b1[:, 0:1]).then_inc(s_hid, 1)
                if not first(s):
                    act.wait_ge(s_prod[1], 4 * (s - 1))
                act.activation(res[:, q, :, 40:41], wt[:, ds(4 * s, 4)].unsqueeze(2), ACT.Copy).then_inc(s_wcol, 1)
                onehots(1, s, q, b_dst)

            steps(act, phase1)
            std()
            ln[0] += 1
            act.wait_ge(s_var, ln[0])
            act.activation(dinv[:, :, :], dinv[:, :, :], ACT.Sqrt).then_inc(s_std, 1)

            for r in range(6):
                act.wait_ge(s_z, r + 1)

                def copy_z(i, half):
                    if not first(i, 1):
                        act.wait_ge(s_mm, NA * r + 8 * i + 4 * half - 4)
                    act.activation(zring[:, 4 * half:4 * half + 4, :], zn[:, ds(8 * i + 4 * half, 4), :],
                                   ACT.Copy).then_inc(s_zr, 1)

                copy_z(0, 0)
                copy_z(0, 1)
                with act.Fori(1, NA // 8) as i:
                    copy_z(i, 0)
                    copy_z(i, 1)
                act.wait_ge(s_mm, NA * r + 20)
                act.activation(zring[:, 0:1, :], zn[:, NA - 1:NA, :], ACT.Copy).then_inc(s_zr, 1)
                act.wait_ge(s_mm, NA * (r + 1))
                act.activation(aggT[:, 1536:NP], ps[:, 3:7, :].rearrange("p b n -> p (b n)")[:, 0:NP - 1536],
                               ACT.Copy).then_inc(s_agga, 1)
                if r == 2:
                    std()
                if r >= 3:
                    act.wait_ge(s_var, 4 + r)
                    act.activation(fsum[:, 3, :], fsum[:, 2, :], ACT.Sqrt).then_inc(s_std, 1)

        @block.tensor
        def _(pe):
            def open_banks(banks):
                for n in banks:
                    mm = pe.matmul(ps[:, n, :], zero_bf[:, 0:P], zero_bf[:, :], start=True, stop=True,
                                   skip_group_check=True)
                return mm

            def merge(d, q):
                pe.wait_ge(s_tri, d + 1)
                if not first(d):
                    pe.wait_ge(s_idx, d - 1)
                o = ps[:, 2 + q, 0:14].rearrange("p (j v) -> p j v", j=2)
                for j in range(2):
                    pe.matmul(o[:, j, 0:1], same_tri[:, q, j, :], ones_bf[:, :], start=(j == 0), stop=False,
                              skip_group_check=True)
                    for i in range(2):
                        lo = 0 if (i, j) == (0, 1) else 1
                        mm = pe.matmul(o[:, j, lo:7], same[:, q, i, j * P:(j + 1) * P],
                                       wparts[:, ds(2 * d + i, 1), lo:7].rearrange("p c v -> p (c v)"),
                                       start=False, stop=(i == 1), skip_group_check=True)
                mm.then_inc(s_ded, 1)

            def scatter(n, s, q, k, width):
                pe.wait_ge(s_oh[n], s + 1)
                pe.wait_ge(s_prod[n], 4 * s + k + 1)
                for half in range(2):
                    mm = pe.matmul(ps[:, half, 0:NA2 * width], onehot[:, q, k, half * P:(half + 1) * P],
                                   prod[:, q, k, 0:NA2 * width], start=False, stop=False, skip_group_check=True)
                mm.then_inc(s_sum[n], 1)

            pe.wait_ge(s_open, 1)
            open_banks(range(2))
            pe.wait_ge(s_edge, 1)

            def phase0(s, q, t):
                merge(s, q)
                for k in range(4):
                    scatter(0, s, q, k, FEAT)

            steps(pe, phase0)

            pe.wait_ge(s_cat, 1)
            for g in range(len(NCOL)):
                if g >= 2:
                    pe.wait_ge(s_catTc, g - 1)
                for a in range(4 * g, min(4 * g + 4, NA)):
                    mm = pe.transpose(ps[0:64, 4 + g % 2, (a % 4) * P:(a % 4 + 1) * P], cat[:, a, :], ident[:, :])
                mm.then_inc(s_catT, 1)
            for n, (c0, w) in enumerate(NCOL):
                pe.wait_ge(s_catTc, n + 1)
                if n >= 2:
                    pe.wait_ge(s_act0, n - 1)
                pe.matmul(ps[:, 6 + n % 2, 0:w], w1T[:, :], catT[:, c0:c0 + w], start=True,
                          stop=True).then_inc(s_h0, 1)
            open_banks(range(2))
            pe.wait_ge(s_norm, 1)
            for a in range(NA):
                bank, col = (4, a) if a < A_LO else (5, a - A_LO)
                mm = pe.matmul(ps[:, bank, col * FEAT:(col + 1) * FEAT], normT[:, a * P:(a + 1) * P], w2T[:, :],
                               start=True, stop=True)
            mm.then_inc(s_out0, 1)

            def radial(s, q, g):
                pe.wait_ge(s_hid, s + 1)
                if not first(s, 1):
                    pe.wait_ge(s_terms, 2 * s - 1 + g)
                for k in (2 * g, 2 * g + 1):
                    mm = pe.matmul(ps[:, 4 + k, 0:384], hidT[:, q, k * P:(k + 1) * P], w2mix[:, :],
                                   start=True, stop=True)
                mm.then_inc(s_rad, 1)

            pe.wait_ge(s_table, 1)
            radial(0, 0, 0)
            radial(0, 0, 1)

            def phase1(s, q, t):
                merge(s + STEPS, q)
                if not after(s):
                    for g in range(2):
                        radial(s + 1, 1 - q, g)
                for k in range(4):
                    scatter(1, s, q, k, MSG)

            steps(pe, phase1)

            def spmm_round(r, norm):
                pe.wait_ge(s_z, r + 1)
                open_banks(range(len(NCOL)))

                def block_times_z(j, landed, copied):
                    pe.wait_ge(s_blk[j % 4], landed)
                    pe.wait_ge(s_zr, copied)
                    g = 32 * (j % 4)
                    for n, (c0, w) in enumerate(NCOL):
                        mm = pe.matmul(ps[g:g + 32, n, 0:w], zring[:, j, :], big[:, j % 4, c0:c0 + w],
                                       start=False, stop=False, skip_group_check=True)
                    mm.then_inc(s_mm, 1)

                with pe.Fori(0, NA // 8) as i:
                    for j in range(8):
                        per = 7 if j % 4 == 0 else 6
                        block_times_z(j, (r * per + i * 2 + j // 4 + 1) * 16, r * 7 + i * 2 + j // 4 + 1)
                block_times_z(0, r * 112 + 112, r * 7 + 7)
                pe.wait_ge(s_aggc, r + 1)
                pe.wait_ge(s_agga, r + 1)
                for a in range(NA):
                    bank, col = (7, a) if a < 16 else (0, a - 16)
                    mm = pe.matmul(ps[:, bank, col * FEAT:(col + 1) * FEAT], aggT[:, a * P:(a + 1) * P],
                                   stack_id[:, :], start=True, stop=True)
                mm.then_inc(s_turn, 1)
                if norm:
                    for i in range(2):
                        pe.wait_ge(s_fs, r * 2 - 6 + i + 1)
                        pe.matmul(ps[:, 1, i * FEAT:(i + 1) * FEAT], ones_f[:, :], fsum[:, 0, :],
                                  start=True, stop=True).then_inc(s_fsp, 1)

            with pe.Fori(0, 3) as r:
                spmm_round(r, False)
            with pe.Fori(3, 6) as r:
                spmm_round(r, True)

        @block.vector
        def _(dve):
            chain = [0]

            def link(ins):
                chain[0] += 1
                ins.then_inc(s_dve, 1)
                dve.wait_ge(s_dve, chain[0])

            def over_f(t):
                return t.unsqueeze(2).broadcast_to([P, NA, FEAT])

            def over_a(t):
                return t.unsqueeze(1).broadcast_to([P, NA, FEAT])

            V = nc.vector
            jobs = [0]

            def std():
                jobs[0] += 1
                dve.wait_ge(s_std, jobs[0])

            def layernorm():
                link(V.tensor_reduce(st[:, 0, :], x[:, :, :], AX, ALU.add))
                link(V.tensor_scalar(st[:, 1, :], st[:, 0, :], 1.0 / FEAT, None, ALU.mult))
                link(V.tensor_tensor(cen[:, :, :], x[:, :, :], over_f(st[:, 1, :]), ALU.subtract))
                link(V.tensor_tensor(sq[:, :, :], cen[:, :, :], cen[:, :, :], ALU.mult))
                link(V.tensor_reduce(st[:, 0, :], sq[:, :, :], AX, ALU.add))
                V.tensor_scalar(st[:, 2, :], st[:, 0, :], 1.0 / FEAT, EPS, ALU.mult, ALU.add).then_inc(s_var, 1)
                std()
                link(V.reciprocal(st[:, 1, :], st[:, 3, :]))
                link(V.tensor_tensor(sq[:, :, :], cen[:, :, :], over_f(st[:, 1, :]), ALU.mult))
                link(V.tensor_scalar(h[:, :, :], sq[:, :, :], 0.0, None, ALU.max))

            V.memset(zero_bf[:, :], 0.0).then_inc(s_open, 1)
            V.memset(ones_bf[:, :], 1.0)
            V.memset(ones_f[:, :], 1.0)
            V.memset(wparts[:, :, 0:2], 1.0)
            V.memset(wparts[:, :, 2:4], 0.0)
            V.memset(res[:, :, :, 41:42], 1.0)
            link(V.memset(hidT[HID1:HID1 + 1, :, :], 1.0))

            dve.wait_ge(s_in["idxT"], 32)
            V.scalar_tensor_tensor(out=keyT, in0=srcT, scalar=float(NP), in1=dstT,
                                   op0=ALU.mult, op1=ALU.add).then_inc(s_keyT, 1)
            dve.wait_ge(s_in["idx"], 32)
            link(V.scalar_tensor_tensor(out=key[:, :], in0=src_i[:, :], scalar=float(NP), in1=dst_i[:, :],
                                        op0=ALU.mult, op1=ALU.add))
            for ids, hi, lo in ((src_i, a_src, b_src), (dst_i, a_dst, b_dst)):
                link(V.tensor_scalar(tmp_i, ids[:, :], 8, None, ALU.arith_shift_right))
                link(V.tensor_copy(hi[:, :], tmp_i))
                link(V.tensor_scalar(tmp_i, ids[:, :], 2 * P - 1, None, ALU.bitwise_and))
                link(V.tensor_copy(lo[:, :], tmp_i))
            dve.wait_ge(s_const, 9)
            link(V.tensor_tensor(to_spare[:, :].rearrange("p (d j) -> p d j", j=2),
                                 spare[:, :].unsqueeze(1).broadcast_to([P, PAIRS, 2]),
                                 key[:, :].rearrange("p (d j) -> p d j", j=2), ALU.subtract))
            dve.wait_ge(s_in["w"], 16)
            link(V.tensor_copy(wparts[:, :, 4], wt[:, :]))
            link(V.tensor_tensor(wrest, wt[:, :], wparts[:, :, 4], ALU.subtract))
            link(V.tensor_copy(wparts[:, :, 5], wrest))
            link(V.tensor_tensor(wrest, wrest, wparts[:, :, 5], ALU.subtract))
            link(V.tensor_copy(wparts[:, :, 6], wrest))
            link(V.tensor_tensor(stack_id[:, :], ident[:, 0:32], ident[:, 32:64], ALU.add))
            link(V.tensor_tensor(stack_id[:, :], stack_id[:, :], ident[:, 64:96], ALU.add))
            link(V.tensor_tensor(stack_id[:, :], stack_id[:, :], ident[:, 96:128], ALU.add))
            dve.wait_ge(s_in["x"], 16)
            layernorm()
            dve.wait_ge(s_in["rel"], 16)
            link(V.tensor_tensor(rel2[:, :, :], rel[:, :, :], rel[:, :, :], ALU.mult))
            V.tensor_reduce(rinv[:, :], rel2[:, :, :], AX, ALU.add).then_inc(s_rlen2, 1)
            dve.wait_ge(s_rlen, 1)
            link(V.reciprocal(rinv[:, :], rlen[:, :]))
            link(V.tensor_tensor(rdir[:, :, 0:2], rel[:, :, 1:3],
                                 rinv[:, :].unsqueeze(2).broadcast_to([P, CH, 2]), ALU.mult))
            V.tensor_tensor(rdir[:, :, 2:5], rel[:, :, :],
                            rinv[:, :].unsqueeze(2).broadcast_to([P, CH, 3]), ALU.mult).then_inc(s_edge, 1)
            dve.wait_ge(s_edge, 1)

            def mark_earlier(d, q):
                dve.wait_ge(s_same, d + 1)
                if not first(d):
                    dve.wait_ge(s_ded, d - 1)
                within = same[:, q, :, :].rearrange("p i (j e) -> p (i j) e", j=2)[:, 0:4:3, :]
                V.tensor_tensor(same_tri[:, q, :, :], within, earlier[:, :].unsqueeze(1).broadcast_to([P, 2, P]),
                                ALU.mult).then_inc(s_tri, 1)

            def entries(d, q):
                dve.wait_ge(s_ded, d + 1)
                if not first(d, 1):
                    dve.wait_ge(s_idx, d)
                m = ps[:, 2 + q, 0:14].rearrange("p (j v) -> p j v", j=2)
                V.tensor_reduce(sc_val[:, ds(d, 1), :, :].rearrange("p d v j -> p (d j) v"),
                                m[:, :, 1:7].rearrange("p j (v i) -> p j v i", i=3), AX, ALU.add)
                V.scalar_tensor_tensor(out=offs[:, :], in0=m[:, :, 0], scalar=0.0, in1=to_spare[:, ds(2 * d, 2)],
                                       op0=ALU.is_gt, op1=ALU.mult).then_inc(s_offs, 1)
                dve.wait_ge(s_offs, d + 1)
                V.tensor_tensor(sc_idx[:, ds(2 * d, 2)], offs[:, :], key[:, ds(2 * d, 2)],
                                ALU.add).then_inc(s_idx, 1)

            def products(n, s, q, k, acol, rows, width):
                if not first(s):
                    dve.wait_ge(s_sum[n], 4 * s - 8 + k + 1)
                V.scalar_tensor_tensor(
                    out=prod[:, q, k, 0:NA2 * width].rearrange("p (a m) -> p a m", a=NA2),
                    in0=iota_a[:, :].unsqueeze(2).broadcast_to([P, NA2, width]), scalar=acol[:, ds(4 * s + k, 1)],
                    in1=rows.unsqueeze(1).broadcast_to([P, NA2, width]),
                    op0=ALU.is_equal, op1=ALU.mult).then_inc(s_prod[n], 1)

            def phase0(s, q, t):
                mark_earlier(s, q)
                dve.wait_ge(s_attr[q], 16 * (t + 1))
                for k in range(4):
                    products(0, s, q, k, a_src, attr[:, q, k, :], FEAT)
                    if k == 2:
                        entries(s, q)

            steps(dve, phase0)

            dve.wait_ge(s_in["wts"], 16 * 12)
            R00, R01, R10 = (w2raw[:, n * 64:(n + 1) * 64].rearrange("h (u v) -> h u v", u=8) for n in range(3))
            R11 = w2raw[:, 192:384].rearrange("h (u v k) -> h u v k", u=8, v=8)
            Q = w2mix[:, 0:256].rearrange("h (o x) -> h o x", o=16)
            AB = w2mix[:, 256:384].rearrange("h (u x) -> h u x", u=8)
            V.tensor_scalar(Q[:, 0:8, 0:8], R10, sqrt(3 / 32), None, ALU.mult)
            V.tensor_scalar(Q[:, 0:8, 8:16], R11[:, :, :, 2], 3 / 8, None, ALU.mult)
            V.tensor_scalar(Q[:, 8:16, 0:8], R00, 0.25, None, ALU.mult)
            V.tensor_scalar(Q[:, 8:16, 8:16], R01, 0.25, None, ALU.mult)
            V.tensor_scalar(AB[:, :, 8:16], R11[:, :, :, 1], sqrt(3) / 8, None, ALU.mult)
            link(V.tensor_scalar(AB[:, :, 0:8], R11[:, :, :, 0], 1 / sqrt(32), None, ALU.mult))
            link(V.scalar_tensor_tensor(out=AB[:, :, 0:8], in0=R11[:, :, :, 2], scalar=-1 / 8, in1=AB[:, :, 0:8],
                                        op0=ALU.mult, op1=ALU.add))

            dve.wait_ge(s_sum[0], CH)
            V.tensor_copy(cat[:, :, 0:32], h[:, :, :])
            for half in range(2):
                rows_of = len(range(half, NA, 2))
                ins = V.tensor_copy(cat[:, half:NA:2, 32:64],
                                    ps[:, half, 0:rows_of * 32].rearrange("p (a f) -> p a f", f=32))
            ins.then_inc(s_cat, 1)
            link(V.tensor_tensor(x[:, :, :], x[:, :, :], over_a(b2b[:, :]), ALU.add))
            for g, (c0, w) in enumerate(NCOL):
                dve.wait_ge(s_catT, g + 1)
                V.tensor_copy(catT[:, c0:c0 + w], ps[0:64, 4 + g % 2, 0:w]).then_inc(s_catTc, 1)
            for n, (c0, w) in enumerate(NCOL):
                dve.wait_ge(s_act0, n + 1)
                ins = V.bn_stats(bnst[:, n, :], actT[:, c0:min(c0 + w, NODES)])
            link(ins)
            link(V.bn_aggr(bnagg[:, 0:2], bnst[:, :, :]))
            V.tensor_scalar(bnagg[:, 2:3], bnagg[:, 1:2], EPS, None, ALU.add).then_inc(s_var, 1)
            std()
            link(V.reciprocal(bnagg[:, 4:5], bnagg[:, 3:4]))
            link(V.tensor_tensor(bnagg[:, 4:5], bnagg[:, 4:5], gamma[:, :], ALU.mult))
            link(V.tensor_tensor(bnagg[:, 5:6], bnagg[:, 0:1], bnagg[:, 4:5], ALU.mult))
            link(V.tensor_tensor(bnagg[:, 5:6], beta[:, :], bnagg[:, 5:6], ALU.subtract))
            V.tensor_scalar(normT, actT, bnagg[:, 4:5], bnagg[:, 5:6], ALU.mult, ALU.add).then_inc(s_norm, 1)
            dve.wait_ge(s_out0, 1)
            for a0, a1, bank in ((0, A_LO, 4), (A_LO, NA, 5)):
                ins = V.tensor_tensor(x[:, a0:a1, :], x[:, a0:a1, :],
                                      ps[:, bank, 0:(a1 - a0) * 32].rearrange("p (a f) -> p a f", f=32), ALU.add)
            link(ins)
            layernorm()
            dve.wait_ge(s_zeroed, 16 * 52)
            link(V.memset(table, 0.0))
            rows = table.rearrange("p a (t c) -> p a t c", c=16)
            comps = h[:, :, 8:32].rearrange("p a (v i) -> p a i v", i=3)
            V.tensor_copy(rows[:, :, 0, 0:8], h[:, :, 0:8])
            V.tensor_copy(rows[:, :, 1:4, 0:8], comps)
            V.tensor_copy(rows[:, :, 4:6, 0:8], comps[:, :, 0:2, :]).then_inc(s_table, 1)

            def phase1(s, q, t):
                mark_earlier(s + STEPS, q)
                dve.wait_ge(s_gath[q], 64 * (t + 1))
                F = gath[:, q, :, :].rearrange("p k (t c) -> p k t c", c=16)
                r3 = rdir[:, ds(4 * s, 4), :]
                V.tensor_tensor(cross1[:, :, :, :], r3[:, :, 1:4].unsqueeze(3).broadcast_to([P, 4, 3, 8]),
                                F[:, :, 3:6, 0:8], ALU.mult)
                V.tensor_tensor(cross2[:, :, :, :], r3[:, :, 2:5].unsqueeze(3).broadcast_to([P, 4, 3, 8]),
                                F[:, :, 2:5, 0:8], ALU.mult).then_inc(s_cross, 1)
                V.tensor_tensor(dots[:, :, :, :].rearrange("p k v i -> p k i v"), F[:, :, 1:4, 0:8],
                                r3[:, :, 0:3].unsqueeze(3).broadcast_to([P, 4, 3, 8]), ALU.mult).then_inc(s_cross, 1)
                dve.wait_ge(s_cross, 2 * s + 1)
                V.tensor_tensor(F[:, :, 1:4, 8:16], cross1[:, :, :, :], cross2[:, :, :, :], ALU.subtract)
                dve.wait_ge(s_cross, 2 * s + 2)
                V.tensor_reduce(F[:, :, 0, 8:16], dots[:, :, :, :], AX, ALU.add).then_inc(s_vec, 1)
                dve.wait_ge(s_vec, s + 1)
                for g in range(2):
                    dve.wait_ge(s_rad, 2 * s + g + 1)
                    T = terms[:, g, :, :]
                    V.tensor_tensor(T[:, :, 0:256].rearrange("p k (o x) -> p k o x", o=16),
                                    ps[:, 4 + 2 * g:6 + 2 * g, 0:256].rearrange("p k (o x) -> p k o x", o=16),
                                    F[:, 2 * g:2 * g + 2, 0, :].unsqueeze(2).broadcast_to([P, 2, 16, 16]), ALU.mult)
                    for k in range(2):
                        ins = V.tensor_tensor(
                            T[:, k, 256:640].rearrange("p (u i x) -> p u i x", u=8, i=3),
                            ps[:, 4 + 2 * g + k, 256:384].rearrange("p (u x) -> p u x", u=8)
                            .unsqueeze(2).broadcast_to([P, 8, 3, 16]),
                            F[:, 2 * g + k, 1:4, :].unsqueeze(1).broadcast_to([P, 8, 3, 16]), ALU.mult)
                    ins.then_inc(s_terms, 1)
                if not first(s):
                    dve.wait_ge(s_prod[1], 4 * (s - 1))
                for g in range(2):
                    dve.wait_ge(s_terms, 2 * s + g + 1)
                    V.tensor_reduce(res[:, q, 2 * g:2 * g + 2, 0:40],
                                    terms[:, g, :, :].rearrange("p k (o x) -> p k o x", x=16), AX,
                                    ALU.add).then_inc(s_red, 1)
                dve.wait_ge(s_red, 2 * s + 2)
                V.tensor_tensor(along[:, :, :, :], res[:, q, :, 0:8].unsqueeze(3).broadcast_to([P, 4, 8, 3]),
                                r3[:, :, 0:3].unsqueeze(2).broadcast_to([P, 4, 8, 3]), ALU.mult).then_inc(s_along, 1)
                dve.wait_ge(s_along, s + 1)
                V.tensor_tensor(res[:, q, :, 16:40], res[:, q, :, 16:40],
                                along[:, :, :, :].rearrange("p k u i -> p k (u i)"), ALU.add).then_inc(s_msg, 1)
                entries(s + STEPS, q)
                dve.wait_ge(s_msg, s + 1)
                dve.wait_ge(s_wcol, s + 1)
                for k in range(4):
                    products(1, s, q, k, a_dst, res[:, q, k, 8:42], MSG)

            steps(dve, phase1)

            dve.wait_ge(s_sum[1], CH)
            for half in range(2):
                rows_of = len(range(half, NA, 2))
                acc = ps[:, half, 0:rows_of * MSG].rearrange("p (a m) -> p a m", m=MSG)
                V.tensor_tensor(x[:, half:NA:2, :], x[:, half:NA:2, :], acc[:, :, 0:32], ALU.add)
                ins = V.tensor_copy(deg[:, half:NA:2, :], acc[:, :, 32:34])
            link(ins)
            layernorm()
            V.tensor_scalar(dinv[:, 0, :], deg[:, :, 0], 1.2e-35, None, ALU.max)
            V.tensor_scalar(dinv[:, 1, :], deg[:, :, 1], 1.0, None, ALU.add).then_inc(s_var, 1)
            std()
            link(V.reciprocal(dinv[:, :, :], dinv[:, :, :]))
            link(V.scalar_tensor_tensor(out=dinv[:, 0, :], in0=deg[:, :, 0], scalar=0.0, in1=dinv[:, 0, :],
                                        op0=ALU.is_gt, op1=ALU.mult))
            link(V.tensor_tensor(dinv[:, 1, :], dinv[:, 1, :], valid[:, :], ALU.mult))
            turned = ((0, 16, 7), (16, NA, 0))

            def part(a0, a1, bank):
                return ps[:, bank, 0:(a1 - a0) * FEAT].rearrange("p (a f) -> p a f", f=FEAT)

            def copy_sums(r):
                dve.wait_ge(s_mm, NA * (r + 1))
                V.tensor_copy(aggT[:, 0:1536], ps[:, 0:3, :].rearrange("p b n -> p (b n)")).then_inc(s_aggc, 1)
                dve.wait_ge(s_turn, r + 1)

            V.tensor_tensor(zn[:, :, :], h[:, :, :], over_f(dinv[:, 0, :]), ALU.mult).then_inc(s_z, 1)
            link(V.tensor_scalar(cen[:, :, :], h[:, :, :], 1.0 - ALPHA, None, ALU.mult))
            for r in range(3):
                copy_sums(r)
                for a0, a1, bank in turned:
                    ins = V.tensor_tensor(sq[:, a0:a1, :], part(a0, a1, bank),
                                          dinv[:, 0, a0:a1].unsqueeze(2).broadcast_to([P, a1 - a0, FEAT]), ALU.mult)
                link(ins)
                link(V.scalar_tensor_tensor(out=h[:, :, :], in0=sq[:, :, :], scalar=ALPHA, in1=cen[:, :, :],
                                            op0=ALU.mult, op1=ALU.add))
                link(V.tensor_scalar(h[:, :, :], h[:, :, :], 0.0, 1.0, ALU.max, ALU.min))
                if r < 2:
                    V.tensor_tensor(zn[:, :, :], h[:, :, :], over_f(dinv[:, 0, :]), ALU.mult).then_inc(s_z, 1)
            link(V.tensor_tensor(x[:, :, :], x[:, :, :], h[:, :, :], ALU.add))
            layernorm()
            V.tensor_tensor(zn[:, :, :], h[:, :, :], over_f(dinv[:, 1, :]), ALU.mult).then_inc(s_z, 1)

            def over_nodes(i, r, src):
                V.tensor_reduce(fsum[:, 0, :], src.rearrange("p a f -> p f a"), AX, ALU.add).then_inc(s_fs, 1)
                dve.wait_ge(s_fsp, 2 * (r - 3) + i + 1)
                return ps[:, 1, i * FEAT:(i + 1) * FEAT]

            for r in range(3, 6):
                copy_sums(r)
                for a0, a1, bank in turned:
                    ins = V.tensor_tensor(sq[:, a0:a1, :], part(a0, a1, bank), zn[:, a0:a1, :], ALU.add)
                link(ins)
                link(V.tensor_tensor(sq[:, :, :], sq[:, :, :], over_f(dinv[:, 1, :]), ALU.mult))
                link(V.tensor_scalar(h[:, :, :], sq[:, :, :], 0.0, None, ALU.max))
                link(V.tensor_scalar(fsum[:, 1, :], over_nodes(0, r, h[:, :, :]), 1.0 / NODES, None, ALU.mult))
                link(V.tensor_tensor(cen[:, :, :], h[:, :, :], over_a(fsum[:, 1, :]), ALU.subtract))
                link(V.tensor_tensor(cen[:, :, :], cen[:, :, :], over_f(valid[:, :]), ALU.mult))
                link(V.tensor_tensor(sq[:, :, :], cen[:, :, :], cen[:, :, :], ALU.mult))
                V.tensor_scalar(fsum[:, 2, :], over_nodes(1, r, sq[:, :, :]), 1.0 / NODES, EPS,
                                ALU.mult, ALU.add).then_inc(s_var, 1)
                std()
                link(V.reciprocal(fsum[:, 4, :], fsum[:, 3, :]))
                link(V.tensor_tensor(fsum[:, 4, :], fsum[:, 4, :], gam3[:, r - 3, :], ALU.mult))
                link(V.tensor_tensor(sq[:, :, :], cen[:, :, :], over_a(fsum[:, 4, :]), ALU.mult))
                link(V.tensor_tensor(h[:, :, :], sq[:, :, :], over_a(bet3[:, r - 3, :]), ALU.add))
                if r < 5:
                    V.tensor_tensor(zn[:, :, :], h[:, :, :], over_f(dinv[:, 1, :]), ALU.mult).then_inc(s_z, 1)
            V.tensor_tensor(x[:, :, :], x[:, :, :], h[:, :, :], ALU.add).then_inc(s_fin, 1)


_INS = [("x", (NP, FEAT)), ("src", (P, CH)), ("dst", (P, CH)), ("srcT", (112, 7 * P)), ("dstT", (112, 7 * P)),
        ("ea3", (P, CH * 3)), ("ea32", (P, CH * FEAT)), ("w", (P, CH)), ("wT", (CH, P)), ("w1T", (64, HID0)),
        ("b1", (HID0, 1)), ("gamma", (HID0, 1)), ("beta", (HID0, 1)), ("w2T", (HID0, FEAT)), ("b2", (1, FEAT)),
        ("l1w1", (HID1, 1)), ("l1b1", (HID1, 1)), ("l1w2", (HID1, 384)), ("l1b2", (1, 384)),
        ("gam3", (1, 3 * FEAT)), ("bet3", (1, 3 * FEAT))]


def kernel(**inputs):
    import numpy as _np
    import concourse.bacc as _bacc
    from concourse.bass_utils import run_bass_kernel_spmd as _run

    i = {k: _np.asarray(v) for k, v in inputs.items()}

    def padded(a, rows, fill):
        return _np.concatenate([a, _np.full((rows - a.shape[0],) + a.shape[1:], fill, a.dtype)])

    src, dst = (padded(i[k], CH * P, NP - 1).reshape(P, CH) for k in ("src", "dst"))
    w = padded(i["edge_weight"], CH * P, 0).reshape(P, CH)
    data = {
        "x": padded(i["x"], NP, 0), "src": src, "dst": dst,
        "srcT": src.T.reshape(112, 7 * P), "dstT": dst.T.reshape(112, 7 * P),
        "ea3": padded(i["edge_attr_3"], CH * P, 1).reshape(P, CH * 3),
        "ea32": padded(i["edge_attr_32"], CH * P, 0).reshape(P, CH * FEAT),
        "w": w, "wT": w.T,
        "w1T": i["L0_gnn_W1"].T, "b1": i["L0_gnn_b1"], "gamma": i["L0_gnn_gamma"], "beta": i["L0_gnn_beta"],
        "w2T": i["L0_gnn_W2"].T, "b2": i["L0_gnn_b2"],
        "l1w1": i["L1_gnn_w1"], "l1b1": i["L1_gnn_b1"], "l1w2": i["L1_gnn_w2"], "l1b2": i["L1_gnn_b2"],
        "gam3": i["L3_gnn_gammas"], "bet3": i["L3_gnn_betas"],
    }
    nc = _bacc.Bacc("TRN2", target_bir_lowering=False, num_devices=1)
    arrays, args = {}, []
    for name, shape in _INS:
        a = _np.ascontiguousarray(data[name].reshape(shape))
        arrays[f"in_{name}"] = a
        args.append(nc.dram_tensor(f"in_{name}", shape, mybir.dt.from_np(a.dtype), kind="ExternalInput").ap())
    args.append(nc.dram_tensor("out_0", (NODES, FEAT), F32, kind="ExternalOutput").ap())
    gnn_program(nc, *args)
    r = _run(nc, [arrays], core_ids=[0])
    return r.results[0]["out_0"]
```

```python
from contextlib import ExitStack
from math import sqrt

import concourse.bass as bass
from concourse import mybir

ALU = mybir.AluOpType
ACT = mybir.ActivationFunctionType
F32 = mybir.dt.float32
BF16 = mybir.dt.bfloat16
I32 = mybir.dt.int32
AX = mybir.AxisListType.X

P = 128
NODES, EDGES, FEAT = 3125, 100000, 32
NA = -(-NODES // P)
NP = NA * P
LAST = NODES - (NA - 1) * P
CH = 784
STEPS = CH // 4
PAIRS = CH // 2
NA2 = -(-NODES // (2 * P))
A_LO = 13
KEPT = 9
RING = NA - KEPT
HID0, HID1 = 128, 64
MSG = 34
ROW = 96
ZERO_PIECES = 20
BEHIND = 3
NCOL = [(n, min(512, NP - n)) for n in range(0, NP, 512)]
EPS = 1e-5
ALPHA = 0.9
BIG = NP * NP


def ds(start, size):
    if isinstance(start, int):
        return slice(start, start + size)
    return bass.ds(start, size)


def gnn_program(nc, x_in, src_in, dst_in, srcT_in, dstT_in, ea3_in, ea32_in, ew_in, ewT_in,
                w1T_in, b1_in, gamma_in, beta_in, w2T_in, b2_in, l1w1_in, l1b1_in, l1w2_in, l1b2_in,
                gam3_in, bet3_in, out):
    with ExitStack() as ctx:
        def sb(name, shape, dt=F32):
            return ctx.enter_context(nc.sbuf_tensor(name, shape, dt))

        def sem(name):
            return ctx.enter_context(nc.semaphore(name))

        adj_w = nc.dram_tensor("adj_w", [BIG + 2 * P, 1], F32, kind="Internal").ap()
        adj_c = nc.dram_tensor("adj_c", [BIG + 2 * P, 1], F32, kind="Internal").ap()
        keys_dram = nc.dram_tensor("keys_dram", [CH, P], F32, kind="Internal").ap()
        feat_dram = nc.dram_tensor("feat_dram", [NP, ROW], F32, kind="Internal").ap()

        ident = sb("ident", [P, P])
        stack_id = sb("stack_id", [P, 32])
        iota_b = sb("iota_b", [P, 2 * P])
        iota_a = sb("iota_a", [P, NA2])
        earlier = sb("earlier", [P, P], BF16)
        spare = sb("spare", [P, 2])
        ones_bf = sb("ones_bf", [P, 1], BF16)
        ones_f = sb("ones_f", [P, P])
        zero_bf = sb("zero_bf", [P, 512], BF16)
        valid = sb("valid", [P, NA])

        kept = sb("kept", [P, KEPT, NP])
        kept_all = kept[:, :, :].rearrange("p k n -> p (k n)")
        placed = [0]

        def edge(*dims, dt=F32, parts=P):
            n = 1
            for d in dims:
                n *= d
            words = n // 2 if dt == BF16 else n
            lo = placed[0]
            placed[0] += words
            assert placed[0] <= KEPT * NP
            v = kept_all[0:parts, lo:lo + words]
            if dt != F32:
                v = v.bitcast(dt)
            if len(dims) == 1:
                return v
            names = ["d%d" % i for i in range(len(dims))]
            return v.rearrange("p (%s) -> p %s" % (" ".join(names), " ".join(names)), **dict(zip(names, dims)))

        src_i = edge(CH, dt=I32)
        dst_i = edge(CH, dt=I32)
        key = edge(CH)
        to_spare = edge(CH)
        a_src = edge(CH)
        b_src = edge(CH)
        a_dst = edge(CH)
        b_dst = edge(CH)
        wt = edge(CH)
        wparts = edge(CH, 7, dt=BF16)
        rlen = edge(CH)
        rinv = edge(CH)
        rdir = edge(CH, 5)
        sc_idx = edge(CH)
        sc_val = edge(PAIRS, 2, 2)
        add_to = sb("add_to", [P, 2, 2], I32)
        add_val = sb("add_val", [P, 2, 2, 2])
        pause = sb("pause", [1, 3])
        take_from = sb("take_from", [P, 2, 4], I32)

        keyrow = edge(2, 2 * P)
        key_gap = edge(2, 2 * P)
        same = edge(2, 2, 2 * P, dt=BF16)
        same_tri = edge(2, 2, P, dt=BF16)
        offs = sb("offs", [P, 2])
        attr = sb("attr", [P, 2, 4, FEAT])
        dist2 = edge(4, 2 * P)
        onehot = edge(2, 4, 2 * P)
        prod = sb("prod", [P, 2, 4, NA2 * MSG + 6])
        wrow = edge(2, 4 * P, parts=HID1)
        hidT = edge(2, 4 * P, parts=HID1 + 1)
        gath = edge(2, 4, ROW)
        cross1 = edge(4, 3, 8)
        cross2 = edge(4, 3, 8)
        dots = edge(4, 8, 3)
        terms = edge(2, 2, 40 * 16)
        res = sb("res", [P, 2, 4, 42])
        along = edge(4, 8, 3)

        w1T = sb("w1T", [64, HID0])
        b1 = sb("b1", [HID0, 1])
        gamma = sb("gamma", [HID0, 1])
        beta = sb("beta", [HID0, 1])
        w2T = sb("w2T", [HID0, FEAT])
        b2b = sb("b2b", [P, FEAT])
        l1w1 = sb("l1w1", [HID1, 1])
        l1b1 = sb("l1b1", [HID1, 1])
        w2raw = sb("w2raw", [HID1 + 1, 384])
        w2mix = sb("w2mix", [HID1 + 1, 384])
        gam3 = sb("gam3", [P, 3, FEAT])
        bet3 = sb("bet3", [P, 3, FEAT])

        x = sb("x", [P, NA, FEAT])
        h = sb("h", [P, NA, FEAT])
        zn = sb("zn", [P, NA, FEAT])
        cen = sb("cen", [P, NA, FEAT])
        sq = sb("sq", [P, NA, FEAT])
        st = sb("st", [P, 4, NA])
        deg = sb("deg", [P, NA, 2])
        dinv = sb("dinv", [P, 2, NA])
        fsum = sb("fsum", [P, 6, FEAT])
        bnst = sb("bnst", [P, len(NCOL), 6])
        bnagg = sb("bnagg", [P, 6])
        zring = sb("zring", [P, 8, FEAT])

        big = sb("big", [P, 4, NP])
        zeros = big[:, 0, :]
        table = big[:, 0, 0:NA * ROW].rearrange("p (a r) -> p a r", a=NA)
        cat = big[:, 1, 0:NA * 64].rearrange("p (a r) -> p a r", a=NA)
        catT = big[0:64, 2, :]
        actT = big[:, 3, :]
        rel = big[:, 1, 0:CH * 3].rearrange("p (c i) -> p c i", i=3)
        rel2 = big[:, 2, 0:CH * 3].rearrange("p (c i) -> p c i", i=3)
        tmp_i = big[:, 3, 0:CH].bitcast(I32)
        wrest = big[:, 3, CH:2 * CH]
        prod_all = prod[:, :, :, :].rearrange("p q k n -> p (q k n)")
        srcT = prod_all[0:112, 0:7 * P].bitcast(I32)
        dstT = prod_all[0:112, 7 * P:14 * P].bitcast(I32)
        keyT = prod_all[0:112, 14 * P:21 * P]
        normT = big[:, 1, :]
        aggT = prod_all[:, 0:NP]

        ps = ctx.enter_context(nc.psum_tensor("ps", [P, 8, 512], F32))

        s_in = {n: sem("in_" + n) for n in ("idx", "idxT", "rel", "w", "x", "wts")}
        s_const = sem("const")
        s_zero = sem("zeros_set")
        s_zeroed = sem("adj_zeroed")
        s_keyT = sem("keyT_ready")
        s_keysd = sem("keys_in_dram")
        s_dve = sem("dve_chain")
        s_edge = sem("edge_data_ready")
        s_rlen2 = sem("rel_sq_ready")
        s_rlen = sem("rel_len_ready")
        s_krow = [sem(f"keyrow{q}") for q in range(2)]
        s_attr = [sem(f"attr{q}") for q in range(2)]
        s_wrow = [sem(f"wrow{q}") for q in range(2)]
        s_gath = [sem(f"gath{q}") for q in range(2)]
        s_gap = sem("key_gap_ready")
        s_same = sem("same_ready")
        s_tri = sem("same_tri_ready")
        s_ded = sem("merged_ready")
        s_offs = sem("offs_ready")
        s_idx = sem("scatter_rows_ready")
        s_addto = sem("add_rows_placed")
        s_addval = sem("add_values_placed")
        s_take = sem("gather_rows_placed")
        s_aw = sem("adj_w_added")
        s_ac = sem("adj_c_added")
        s_dist = [sem(f"p{n}_dist_ready") for n in range(2)]
        s_oh = [sem(f"p{n}_onehot_ready") for n in range(2)]
        s_prod = [sem(f"p{n}_prod_ready") for n in range(2)]
        s_sum = [sem(f"p{n}_chunk_summed") for n in range(2)]
        s_open = sem("acc_open")
        s_hid = sem("hidden_ready")
        s_rad = sem("radial_ready")
        s_radfree = sem("radial_used")
        s_cross = sem("cross_terms_ready")
        s_vec = sem("vectors_ready")
        s_terms = sem("terms_ready")
        s_red = sem("terms_summed")
        s_along = sem("along_ready")
        s_msg = sem("messages_ready")
        s_wcol = sem("weight_column_ready")
        s_var = sem("var_ready")
        s_std = sem("std_ready")
        s_cat = sem("cat_ready")
        s_catT = sem("catT_in_psum")
        s_catTc = sem("catT_copied")
        s_h0 = sem("hidden0_in_psum")
        s_act0 = sem("act0_ready")
        s_norm = sem("norm0_ready")
        s_out0 = sem("out0_in_psum")
        s_w2 = sem("w2mix_ready")
        s_table = sem("table_ready")
        s_feat = sem("feat_in_dram")
        s_z = sem("z_ready")
        s_zr = sem("zring_ready")
        s_blk = [sem(f"adj_block{q}") for q in range(4)]
        s_kept = sem("kept_blocks")
        s_mm = sem("block_used")
        s_aggc = sem("agg_copied")
        s_agga = sem("agg_copied_act")
        s_turn = sem("agg_turned")
        s_fs = sem("feature_sums")
        s_fsp = sem("feature_sums_in_psum")
        s_fin = sem("result_ready")
        s_out = sem("out_stored")

        def steps(eng, body):
            for s in range(2):
                body(s, s, 0)
            with eng.Fori(1, STEPS // 2 - 1) as t:
                for q in range(2):
                    body(t * 2 + q, q, t)
            for s in range(STEPS - 2, STEPS):
                body(s, s % 2, s // 2)

        def first(s, n=2):
            return isinstance(s, int) and s < n

        def after(s, n=1):
            return isinstance(s, int) and s >= STEPS - n

        block = ctx.enter_context(nc.Block())

        @block.sync
        def _(sp):
            sp.dma_start(srcT, srcT_in).then_inc(s_in["idxT"], 16)
            sp.dma_start(dstT, dstT_in).then_inc(s_in["idxT"], 16)
            sp.dma_start(src_i[:, :], src_in).then_inc(s_in["idx"], 16)
            sp.dma_start(dst_i[:, :], dst_in).then_inc(s_in["idx"], 16)
            sp.dma_start(wt[:, :], ew_in).then_inc(s_in["w"], 16)
            sp.dma_start(x[:, :, :], x_in.rearrange("(a b) f -> b a f", b=P)).then_inc(s_in["x"], 16)
            sp.dma_start(rel[:, :, :], ea3_in).then_inc(s_in["rel"], 16)
            loads = [(w1T[:, :], w1T_in), (b1[:, :], b1_in), (gamma[:, :], gamma_in), (beta[:, :], beta_in),
                     (w2T[:, :], w2T_in), (b2b[:, :], b2_in.broadcast_to([P, FEAT])),
                     (l1w1[:, :], l1w1_in), (l1b1[:, :], l1b1_in),
                     (w2raw[0:HID1, :], l1w2_in), (w2raw[HID1:HID1 + 1, :], l1b2_in),
                     (gam3[:, :, :], gam3_in.broadcast_to([P, 3 * FEAT]).rearrange("p (l f) -> p l f", l=3)),
                     (bet3[:, :, :], bet3_in.broadcast_to([P, 3 * FEAT]).rearrange("p (l f) -> p l f", l=3))]
            for dst, src in loads:
                sp.dma_start(dst, src).then_inc(s_in["wts"], 16)

            sp.wait_ge(s_keyT, 1)
            sp.dma_start(keys_dram.rearrange("(q j) p -> q (j p)", j=7), keyT).then_inc(s_keysd, 16)
            sp.wait_ge(s_keysd, 16)

            def load_keys(d, q):
                if not first(d):
                    sp.wait_ge(s_gap, 2 * (d - 1))
                row = keys_dram[ds(2 * d, 2), :].rearrange("(o c) p -> o (c p)", o=1)
                sp.dma_start(keyrow[:, q, :], row.broadcast_to([P, 2 * P])).then_inc(s_krow[q], 16)

            def load0(s, q, t):
                load_keys(s, q)
                if not first(s):
                    sp.wait_ge(s_prod[0], 4 * (s - 1))
                sp.dma_start(attr[:, q, :, :].rearrange("p k f -> p (k f)"),
                             ea32_in[:, ds(s * (4 * FEAT), 4 * FEAT)]).then_inc(s_attr[q], 16)

            steps(sp, load0)
            sp.wait_ge(s_table, 1)
            sp.dma_start(feat_dram.rearrange("(a b) r -> b a r", b=P), table).then_inc(s_feat, 16)

            def load1(s, q, t):
                load_keys(s + STEPS, q)
                if not first(s):
                    sp.wait_ge(s_hid, s - 1)
                row = ewT_in[ds(4 * s, 4), :].rearrange("(o c) p -> o (c p)", o=1)
                sp.dma_start(wrow[:, q, :], row.broadcast_to([HID1, 4 * P])).then_inc(s_wrow[q], 16)

            steps(sp, load1)

            sp.wait_ge(s_aw, 32 * PAIRS)
            sp.wait_ge(s_ac, 32 * PAIRS)
            sp.wait_ge(s_feat, 16)
            sp.wait_ge(s_sum[1], CH)

            def load_round(r, adj):
                for i in range(RING):
                    if i >= 12:
                        sp.wait_ge(s_mm, r * NA + (i + KEPT - 3))
                    elif i >= 4:
                        sp.wait_ge(s_mm, r * NA + (i - 3))
                    elif not first(r, 1):
                        sp.wait_ge(s_mm, r * NA + (i - 3))
                    m = i if i < RING // 2 else i + KEPT
                    sp.dma_start(big[:, i % 4, :], adj[m * P:(m + 1) * P, :]).then_inc(s_blk[i % 4], 16)

            for layer, sums in enumerate((adj_w, adj_c)):
                adj = sums[0:BIG, :].rearrange("(s d) o -> s (d o)", d=NP)
                if layer == 1:
                    sp.wait_ge(s_mm, 2 * NA + RING // 2 + KEPT)
                for c in range(KEPT):
                    m = RING // 2 + c
                    sp.dma_start(kept[:, c, :], adj[m * P:(m + 1) * P, :]).then_inc(s_kept, 16)
                load_round(3 * layer, adj)
                with sp.Fori(3 * layer + 1, 3 * layer + 3) as r:
                    load_round(r, adj)

            sp.wait_ge(s_fin, 1)
            sp.dma_start(out[0:(NA - 1) * P, :].rearrange("(a b) f -> b a f", b=P),
                         x[:, 0:NA - 1, :]).then_inc(s_out, 16)
            sp.dma_start(out[(NA - 1) * P:NODES, :], x[0:LAST, NA - 1, :]).then_inc(s_out, 16)
            sp.wait_ge(s_out, 32)

        @block.gpsimd
        def _(pool):
            pool.memset(zeros, 0.0).then_inc(s_zero, 1)
            pool.memset(ident[:, :], 0.0).then_inc(s_const, 1)
            pool.memset(earlier[:, :], 1.0).then_inc(s_const, 1)
            pool.memset(valid[:, :], 1.0).then_inc(s_const, 1)
            pool.wait_ge(s_const, 3)
            pool.affine_select(out=ident[:, :], in_=ident[:, :], compare_op=ALU.not_equal, fill=1.0,
                               base=0, pattern=[[-1, P]], channel_multiplier=1).then_inc(s_const, 1)
            pool.affine_select(out=earlier[:, :], in_=earlier[:, :], compare_op=ALU.is_gt, fill=0.0,
                               base=0, pattern=[[1, P]], channel_multiplier=-1).then_inc(s_const, 1)
            pool.affine_select(out=valid[:, :], in_=valid[:, :], compare_op=ALU.is_gt, fill=0.0,
                               base=NODES, pattern=[[-P, NA]], channel_multiplier=-1).then_inc(s_const, 1)
            pool.iota(iota_b[:, :], [[1, 2 * P]], base=0, channel_multiplier=0,
                      allow_small_or_imprecise_dtypes=True).then_inc(s_const, 1)
            pool.iota(iota_a[:, :], [[1, NA2]], base=0, channel_multiplier=0,
                      allow_small_or_imprecise_dtypes=True).then_inc(s_const, 1)
            pool.iota(spare[:, :], [[P, 2]], base=BIG, channel_multiplier=1,
                      allow_small_or_imprecise_dtypes=True).then_inc(s_const, 1)

            last_entry = pool.to_reg(BIG + 2 * P - 1)
            last_node = pool.to_reg(NP - 1)

            def snap(v):
                return v if isinstance(v, int) else pool.snap(v)

            def hold_for_waits(n):
                pool.tensor_tensor(pause[:, n:n + 1], spare[0:1, 0:1], spare[0:1, 1:2], ALU.add)

            def add_pair(d, q):
                ready, landed = snap(d + 1), snap(d * 32)
                idx, val = sc_idx[:, ds(2 * d, 2)], sc_val[:, ds(d, 1), :, :].rearrange("p d v j -> p (d v) j")
                pool.wait_ge(s_idx, ready)
                pool.tensor_copy(add_to[:, q, :], idx).then_inc(s_addto, 1)
                pool.tensor_copy(add_val[:, q, :, :], val).then_inc(s_addval, 1)
                pool.wait_ge(s_addto, ready)
                pool.wait_ge(s_addval, ready)
                for v, (adj, done) in enumerate(((adj_c, s_ac), (adj_w, s_aw))):
                    if not first(d, 1):
                        pool.wait_ge(done, landed)
                    hold_for_waits(v)
                    for j in range(2):
                        pool.indirect_dma_start(adj, bass.IndirectOffsetOnAxis(ap=add_to[:, q, j:j + 1], axis=0),
                                                add_val[:, q, v, j:j + 1], None, bounds_check=last_entry,
                                                compute_op=ALU.add).then_inc(done, 16)

            pool.wait_ge(s_zeroed, 16 * (2 * ZERO_PIECES + 2))

            add_pair(0, 0)
            with pool.Fori(0, (STEPS - BEHIND - 1) // 2) as t:
                add_pair(t * 2 + 1, 1)
                add_pair(t * 2 + 2, 0)
            pool.wait_ge(s_feat, 16)

            def gather(s, q):
                used, taken, rows = snap(2 * (s - 1)) if not first(s) else 0, snap(s + 1), src_i[:, ds(4 * s, 4)]
                if not first(s):
                    pool.wait_ge(s_terms, used)
                pool.tensor_copy(take_from[:, q, :], rows).then_inc(s_take, 1)
                pool.wait_ge(s_take, taken)
                hold_for_waits(2)
                for k in range(4):
                    pool.indirect_dma_start(gath[:, q, k, :], None, feat_dram,
                                            bass.IndirectOffsetOnAxis(ap=take_from[:, q, k:k + 1], axis=0),
                                            bounds_check=last_node).then_inc(s_gath[q], 16)

            gather(0, 0)

            def phase1(s, q, t):
                if not after(s):
                    gather(s + 1, 1 - q)
                add_pair(s + (STEPS - BEHIND), 1 - q)

            steps(pool, phase1)
            for d in range(PAIRS - BEHIND, PAIRS):
                add_pair(d, d % 2)

        @block.scalar
        def _(act):
            act.wait_ge(s_zero, 1)
            for adj in (adj_w, adj_c):
                act.dma_start(adj[BIG:BIG + 2 * P, :].rearrange("(p c) o -> p (c o)", p=P),
                              zeros[:, 0:2]).then_inc(s_zeroed, 16)

            def zero_piece(t, adj):
                act.dma_start(adj[ds(t * (BIG // ZERO_PIECES), BIG // ZERO_PIECES), :]
                              .rearrange("(p i c) o -> p i (c o)", p=P, i=2),
                              zeros[:, 0:BIG // ZERO_PIECES // P // 2].unsqueeze(1)
                              .broadcast_to([P, 2, BIG // ZERO_PIECES // P // 2])).then_inc(s_zeroed, 16)

            ln = [0]

            def std():
                ln[0] += 1
                act.wait_ge(s_var, ln[0])
                act.activation(st[:, 3, :], st[:, 2, :], ACT.Sqrt).then_inc(s_std, 1)

            std()
            act.wait_ge(s_rlen2, 1)
            act.activation(rlen[:, :], rinv[:, :], ACT.Sqrt).then_inc(s_rlen, 1)
            act.wait_ge(s_const, 9)

            def compare(d, q):
                act.wait_ge(s_krow[q], d * 8 - q * 8 + 16)
                if not first(d, 1):
                    act.wait_ge(s_same, d)
                for i in range(2):
                    act.activation(key_gap[:, i, :], keyrow[:, q, :], ACT.Square, scale=-1.0,
                                   bias=key[:, ds(2 * d + i, 1)]).then_inc(s_gap, 1)
                act.wait_ge(s_gap, 2 * d + 2)
                if not first(d):
                    act.wait_ge(s_ded, d - 1)
                act.activation(same[:, q, :, :], key_gap[:, :, :], ACT.Relu, scale=-1.0,
                               bias=1.0).then_inc(s_same, 1)

            def onehots(n, s, q, bcol):
                if not first(s, 1):
                    act.wait_ge(s_oh[n], s)
                for k in range(4):
                    act.activation(dist2[:, k, :], iota_b[:, :], ACT.Square, scale=-1.0,
                                   bias=bcol[:, ds(4 * s + k, 1)]).then_inc(s_dist[n], 1)
                act.wait_ge(s_dist[n], 4 * (s + 1))
                if not first(s):
                    act.wait_ge(s_sum[n], 4 * (s - 1))
                act.activation(onehot[:, q, :, :], dist2[:, :, :], ACT.Relu, scale=-1.0,
                               bias=1.0).then_inc(s_oh[n], 1)

            act.wait_ge(s_edge, 1)

            def phase0(s, q, t):
                compare(s, q)
                onehots(0, s, q, b_src)

            def phase0_and_zeros(s, q, t):
                zero_piece(t, (adj_w, adj_c)[q])
                phase0(s, q, t)

            for q in range(2):
                phase0_and_zeros(q, q, 0)
            with act.Fori(1, ZERO_PIECES) as t:
                for q in range(2):
                    phase0_and_zeros(t * 2 + q, q, t)
            with act.Fori(ZERO_PIECES, STEPS // 2) as t:
                for q in range(2):
                    phase0(t * 2 + q, q, t)

            for n, (c0, w) in enumerate(NCOL):
                act.wait_ge(s_h0, n + 1)
                act.activation(actT[:, c0:c0 + w], ps[:, 6 + n % 2, 0:w], ACT.Relu,
                               bias=b1[:, 0:1]).then_inc(s_act0, 1)
            act.wait_ge(s_var, 2)
            act.activation(bnagg[:, 3:4], bnagg[:, 2:3], ACT.Sqrt).then_inc(s_std, 1)
            ln[0] += 1
            std()

            def phase1(s, q, t):
                compare(s + STEPS, q)
                act.wait_ge(s_wrow[q], 16 * (t + 1))
                if not first(s):
                    act.wait_ge(s_rad, 2 * (s - 1))
                act.activation(hidT[0:HID1, q, :], wrow[:, q, :], ACT.Relu, scale=l1w1[:, 0:1],
                               bias=l1b1[:, 0:1]).then_inc(s_hid, 1)
                if not first(s):
                    act.wait_ge(s_prod[1], 4 * (s - 1))
                act.activation(res[:, q, :, 40:41], wt[:, ds(4 * s, 4)].unsqueeze(2), ACT.Copy).then_inc(s_wcol, 1)
                onehots(1, s, q, b_dst)

            steps(act, phase1)
            std()
            ln[0] += 1
            act.wait_ge(s_var, ln[0])
            act.activation(dinv[:, :, :], dinv[:, :, :], ACT.Sqrt).then_inc(s_std, 1)

            for r in range(6):
                act.wait_ge(s_z, r + 1)

                def copy_z(i, half):
                    if not first(i, 1):
                        act.wait_ge(s_mm, NA * r + 8 * i + 4 * half - 4)
                    act.activation(zring[:, 4 * half:4 * half + 4, :], zn[:, ds(8 * i + 4 * half, 4), :],
                                   ACT.Copy).then_inc(s_zr, 1)

                copy_z(0, 0)
                copy_z(0, 1)
                with act.Fori(1, NA // 8) as i:
                    copy_z(i, 0)
                    copy_z(i, 1)
                act.wait_ge(s_mm, NA * r + 20)
                act.activation(zring[:, 0:1, :], zn[:, NA - 1:NA, :], ACT.Copy).then_inc(s_zr, 1)
                act.wait_ge(s_mm, NA * (r + 1))
                act.activation(aggT[:, 1536:NP], ps[:, 3:7, :].rearrange("p b n -> p (b n)")[:, 0:NP - 1536],
                               ACT.Copy).then_inc(s_agga, 1)
                if r == 2:
                    std()
                if r >= 3:
                    act.wait_ge(s_var, 4 + r)
                    act.activation(fsum[:, 3, :], fsum[:, 2, :], ACT.Sqrt).then_inc(s_std, 1)

        @block.tensor
        def _(pe):
            def open_banks(banks):
                for n in banks:
                    mm = pe.matmul(ps[:, n, :], zero_bf[:, 0:P], zero_bf[:, :], start=True, stop=True,
                                   skip_group_check=True)
                return mm

            def merge(d, q):
                pe.wait_ge(s_tri, d + 1)
                if not first(d):
                    pe.wait_ge(s_idx, d - 1)
                o = ps[:, 2 + q, 0:14].rearrange("p (j v) -> p j v", j=2)
                for j in range(2):
                    pe.matmul(o[:, j, 0:1], same_tri[:, q, j, :], ones_bf[:, :], start=(j == 0), stop=False,
                              skip_group_check=True)
                    for i in range(2):
                        lo = 0 if (i, j) == (0, 1) else 1
                        mm = pe.matmul(o[:, j, lo:7], same[:, q, i, j * P:(j + 1) * P],
                                       wparts[:, ds(2 * d + i, 1), lo:7].rearrange("p c v -> p (c v)"),
                                       start=False, stop=(i == 1), skip_group_check=True)
                mm.then_inc(s_ded, 1)

            def scatter(n, s, q, k, width):
                pe.wait_ge(s_oh[n], s + 1)
                pe.wait_ge(s_prod[n], 4 * s + k + 1)
                for half in range(2):
                    mm = pe.matmul(ps[:, half, 0:NA2 * width], onehot[:, q, k, half * P:(half + 1) * P],
                                   prod[:, q, k, 0:NA2 * width], start=False, stop=False, skip_group_check=True)
                mm.then_inc(s_sum[n], 1)

            pe.wait_ge(s_open, 1)
            open_banks(range(2))
            pe.wait_ge(s_edge, 1)

            def phase0(s, q, t):
                merge(s, q)
                for k in range(4):
                    scatter(0, s, q, k, FEAT)

            steps(pe, phase0)

            pe.wait_ge(s_cat, 1)
            for g in range(len(NCOL)):
                if g >= 2:
                    pe.wait_ge(s_catTc, g - 1)
                for a in range(4 * g, min(4 * g + 4, NA)):
                    mm = pe.transpose(ps[0:64, 4 + g % 2, (a % 4) * P:(a % 4 + 1) * P], cat[:, a, :], ident[:, :])
                mm.then_inc(s_catT, 1)
            for n, (c0, w) in enumerate(NCOL):
                pe.wait_ge(s_catTc, n + 1)
                if n >= 2:
                    pe.wait_ge(s_act0, n - 1)
                pe.matmul(ps[:, 6 + n % 2, 0:w], w1T[:, :], catT[:, c0:c0 + w], start=True,
                          stop=True).then_inc(s_h0, 1)
            open_banks(range(2))
            pe.wait_ge(s_norm, 1)
            for a in range(NA):
                bank, col = (4, a) if a < A_LO else (5, a - A_LO)
                mm = pe.matmul(ps[:, bank, col * FEAT:(col + 1) * FEAT], normT[:, a * P:(a + 1) * P], w2T[:, :],
                               start=True, stop=True)
            mm.then_inc(s_out0, 1)

            def radial(s, q, g):
                pe.wait_ge(s_hid, s + 1)
                if not first(s, 1):
                    pe.wait_ge(s_terms, 2 * s - 1 + g)
                for k in (2 * g, 2 * g + 1):
                    mm = pe.matmul(ps[:, 4 + k, 0:384], hidT[:, q, k * P:(k + 1) * P], w2mix[:, :],
                                   start=True, stop=True)
                mm.then_inc(s_rad, 1)

            pe.wait_ge(s_table, 1)
            radial(0, 0, 0)
            radial(0, 0, 1)

            def phase1(s, q, t):
                merge(s + STEPS, q)
                if not after(s):
                    for g in range(2):
                        radial(s + 1, 1 - q, g)
                for k in range(4):
                    scatter(1, s, q, k, MSG)

            steps(pe, phase1)

            def spmm_round(r, norm):
                pe.wait_ge(s_z, r + 1)
                open_banks(range(len(NCOL)))

                def block_times_z(m, values):
                    pe.wait_ge(s_zr, r * 7 + (m // 4 + 1))
                    g = 32 * (m % 4)
                    for n, (c0, w) in enumerate(NCOL):
                        mm = pe.matmul(ps[g:g + 32, n, 0:w], zring[:, m % 8, :], values[:, c0:c0 + w],
                                       start=False, stop=False, skip_group_check=True)
                    mm.then_inc(s_mm, 1)

                def ring_block(i):
                    m = i if i < RING // 2 else i + KEPT
                    pe.wait_ge(s_blk[i % 4], r * (RING // 4 * 16) + (i // 4 + 1) * 16)
                    block_times_z(m, big[:, i % 4, :])

                for i in range(RING // 2):
                    ring_block(i)
                pe.wait_ge(s_kept, 16 * KEPT * (2 if norm else 1))
                for c in range(KEPT):
                    block_times_z(RING // 2 + c, kept[:, c, :])
                for i in range(RING // 2, RING):
                    ring_block(i)
                pe.wait_ge(s_aggc, r + 1)
                pe.wait_ge(s_agga, r + 1)
                for a in range(NA):
                    bank, col = (7, a) if a < 16 else (0, a - 16)
                    mm = pe.matmul(ps[:, bank, col * FEAT:(col + 1) * FEAT], aggT[:, a * P:(a + 1) * P],
                                   stack_id[:, :], start=True, stop=True)
                mm.then_inc(s_turn, 1)
                if norm:
                    for i in range(2):
                        pe.wait_ge(s_fs, r * 2 - 6 + i + 1)
                        pe.matmul(ps[:, 1, i * FEAT:(i + 1) * FEAT], ones_f[:, :], fsum[:, 0, :],
                                  start=True, stop=True).then_inc(s_fsp, 1)

            with pe.Fori(0, 3) as r:
                spmm_round(r, False)
            with pe.Fori(3, 6) as r:
                spmm_round(r, True)

        @block.vector
        def _(dve):
            chain = [0]

            def link(ins):
                chain[0] += 1
                ins.then_inc(s_dve, 1)
                dve.wait_ge(s_dve, chain[0])

            def over_f(t):
                return t.unsqueeze(2).broadcast_to([P, NA, FEAT])

            def over_a(t):
                return t.unsqueeze(1).broadcast_to([P, NA, FEAT])

            V = nc.vector
            jobs = [0]

            def std():
                jobs[0] += 1
                dve.wait_ge(s_std, jobs[0])

            def layernorm():
                link(V.tensor_reduce(st[:, 0, :], x[:, :, :], AX, ALU.add))
                link(V.tensor_scalar(st[:, 1, :], st[:, 0, :], 1.0 / FEAT, None, ALU.mult))
                link(V.tensor_tensor(cen[:, :, :], x[:, :, :], over_f(st[:, 1, :]), ALU.subtract))
                link(V.tensor_tensor(sq[:, :, :], cen[:, :, :], cen[:, :, :], ALU.mult))
                link(V.tensor_reduce(st[:, 0, :], sq[:, :, :], AX, ALU.add))
                V.tensor_scalar(st[:, 2, :], st[:, 0, :], 1.0 / FEAT, EPS, ALU.mult, ALU.add).then_inc(s_var, 1)
                std()
                link(V.reciprocal(st[:, 1, :], st[:, 3, :]))
                link(V.tensor_tensor(sq[:, :, :], cen[:, :, :], over_f(st[:, 1, :]), ALU.mult))
                link(V.tensor_scalar(h[:, :, :], sq[:, :, :], 0.0, None, ALU.max))

            V.memset(zero_bf[:, :], 0.0).then_inc(s_open, 1)
            V.memset(ones_bf[:, :], 1.0)
            V.memset(ones_f[:, :], 1.0)
            V.memset(wparts[:, :, 0:2], 1.0)
            V.memset(wparts[:, :, 2:4], 0.0)
            V.memset(res[:, :, :, 41:42], 1.0)
            link(V.memset(hidT[HID1:HID1 + 1, :, :], 1.0))

            dve.wait_ge(s_in["idxT"], 32)
            V.scalar_tensor_tensor(out=keyT, in0=srcT, scalar=float(NP), in1=dstT,
                                   op0=ALU.mult, op1=ALU.add).then_inc(s_keyT, 1)
            dve.wait_ge(s_in["idx"], 32)
            link(V.scalar_tensor_tensor(out=key[:, :], in0=src_i[:, :], scalar=float(NP), in1=dst_i[:, :],
                                        op0=ALU.mult, op1=ALU.add))
            for ids, hi, lo in ((src_i, a_src, b_src), (dst_i, a_dst, b_dst)):
                link(V.tensor_scalar(tmp_i, ids[:, :], 8, None, ALU.arith_shift_right))
                link(V.tensor_copy(hi[:, :], tmp_i))
                link(V.tensor_scalar(tmp_i, ids[:, :], 2 * P - 1, None, ALU.bitwise_and))
                link(V.tensor_copy(lo[:, :], tmp_i))
            dve.wait_ge(s_const, 9)
            link(V.tensor_tensor(to_spare[:, :].rearrange("p (d j) -> p d j", j=2),
                                 spare[:, :].unsqueeze(1).broadcast_to([P, PAIRS, 2]),
                                 key[:, :].rearrange("p (d j) -> p d j", j=2), ALU.subtract))
            dve.wait_ge(s_in["w"], 16)
            link(V.tensor_copy(wparts[:, :, 4], wt[:, :]))
            link(V.tensor_tensor(wrest, wt[:, :], wparts[:, :, 4], ALU.subtract))
            link(V.tensor_copy(wparts[:, :, 5], wrest))
            link(V.tensor_tensor(wrest, wrest, wparts[:, :, 5], ALU.subtract))
            link(V.tensor_copy(wparts[:, :, 6], wrest))
            link(V.tensor_tensor(stack_id[:, :], ident[:, 0:32], ident[:, 32:64], ALU.add))
            link(V.tensor_tensor(stack_id[:, :], stack_id[:, :], ident[:, 64:96], ALU.add))
            link(V.tensor_tensor(stack_id[:, :], stack_id[:, :], ident[:, 96:128], ALU.add))
            dve.wait_ge(s_in["x"], 16)
            layernorm()
            dve.wait_ge(s_in["rel"], 16)
            link(V.tensor_tensor(rel2[:, :, :], rel[:, :, :], rel[:, :, :], ALU.mult))
            V.tensor_reduce(rinv[:, :], rel2[:, :, :], AX, ALU.add).then_inc(s_rlen2, 1)
            dve.wait_ge(s_rlen, 1)
            link(V.reciprocal(rinv[:, :], rlen[:, :]))
            link(V.tensor_tensor(rdir[:, :, 0:2], rel[:, :, 1:3],
                                 rinv[:, :].unsqueeze(2).broadcast_to([P, CH, 2]), ALU.mult))
            V.tensor_tensor(rdir[:, :, 2:5], rel[:, :, :],
                            rinv[:, :].unsqueeze(2).broadcast_to([P, CH, 3]), ALU.mult).then_inc(s_edge, 1)
            dve.wait_ge(s_edge, 1)

            def mark_earlier(d, q):
                dve.wait_ge(s_same, d + 1)
                if not first(d):
                    dve.wait_ge(s_ded, d - 1)
                within = same[:, q, :, :].rearrange("p i (j e) -> p (i j) e", j=2)[:, 0:4:3, :]
                V.tensor_tensor(same_tri[:, q, :, :], within, earlier[:, :].unsqueeze(1).broadcast_to([P, 2, P]),
                                ALU.mult).then_inc(s_tri, 1)

            def entries(d, q):
                dve.wait_ge(s_ded, d + 1)
                if not first(d, 1):
                    dve.wait_ge(s_idx, d)
                m = ps[:, 2 + q, 0:14].rearrange("p (j v) -> p j v", j=2)
                V.tensor_reduce(sc_val[:, ds(d, 1), :, :].rearrange("p d v j -> p (d j) v"),
                                m[:, :, 1:7].rearrange("p j (v i) -> p j v i", i=3), AX, ALU.add)
                V.scalar_tensor_tensor(out=offs[:, :], in0=m[:, :, 0], scalar=0.0, in1=to_spare[:, ds(2 * d, 2)],
                                       op0=ALU.is_gt, op1=ALU.mult).then_inc(s_offs, 1)

            def entry_places(d):
                dve.wait_ge(s_offs, d + 1)
                V.tensor_tensor(sc_idx[:, ds(2 * d, 2)], offs[:, :], key[:, ds(2 * d, 2)],
                                ALU.add).then_inc(s_idx, 1)

            def products(n, s, q, k, acol, rows, width):
                if not first(s):
                    dve.wait_ge(s_sum[n], 4 * s - 8 + k + 1)
                V.scalar_tensor_tensor(
                    out=prod[:, q, k, 0:NA2 * width].rearrange("p (a m) -> p a m", a=NA2),
                    in0=iota_a[:, :].unsqueeze(2).broadcast_to([P, NA2, width]), scalar=acol[:, ds(4 * s + k, 1)],
                    in1=rows.unsqueeze(1).broadcast_to([P, NA2, width]),
                    op0=ALU.is_equal, op1=ALU.mult).then_inc(s_prod[n], 1)

            def phase0(s, q, t):
                mark_earlier(s, q)
                dve.wait_ge(s_attr[q], 16 * (t + 1))
                for k in range(4):
                    products(0, s, q, k, a_src, attr[:, q, k, :], FEAT)
                    if k == 2:
                        entries(s, q)
                entry_places(s)

            steps(dve, phase0)

            dve.wait_ge(s_in["wts"], 16 * 12)
            R00, R01, R10 = (w2raw[:, n * 64:(n + 1) * 64].rearrange("h (u v) -> h u v", u=8) for n in range(3))
            R11 = w2raw[:, 192:384].rearrange("h (u v k) -> h u v k", u=8, v=8)
            Q = w2mix[:, 0:256].rearrange("h (o x) -> h o x", o=16)
            AB = w2mix[:, 256:384].rearrange("h (u x) -> h u x", u=8)
            V.tensor_scalar(Q[:, 0:8, 0:8], R10, sqrt(3 / 32), None, ALU.mult)
            V.tensor_scalar(Q[:, 0:8, 8:16], R11[:, :, :, 2], 3 / 8, None, ALU.mult)
            V.tensor_scalar(Q[:, 8:16, 0:8], R00, 0.25, None, ALU.mult)
            V.tensor_scalar(Q[:, 8:16, 8:16], R01, 0.25, None, ALU.mult)
            V.tensor_scalar(AB[:, :, 8:16], R11[:, :, :, 1], sqrt(3) / 8, None, ALU.mult)
            link(V.tensor_scalar(AB[:, :, 0:8], R11[:, :, :, 0], 1 / sqrt(32), None, ALU.mult))
            link(V.scalar_tensor_tensor(out=AB[:, :, 0:8], in0=R11[:, :, :, 2], scalar=-1 / 8, in1=AB[:, :, 0:8],
                                        op0=ALU.mult, op1=ALU.add))

            dve.wait_ge(s_sum[0], CH)
            V.tensor_copy(cat[:, :, 0:32], h[:, :, :])
            for half in range(2):
                rows_of = len(range(half, NA, 2))
                ins = V.tensor_copy(cat[:, half:NA:2, 32:64],
                                    ps[:, half, 0:rows_of * 32].rearrange("p (a f) -> p a f", f=32))
            ins.then_inc(s_cat, 1)
            link(V.tensor_tensor(x[:, :, :], x[:, :, :], over_a(b2b[:, :]), ALU.add))
            for g, (c0, w) in enumerate(NCOL):
                dve.wait_ge(s_catT, g + 1)
                V.tensor_copy(catT[:, c0:c0 + w], ps[0:64, 4 + g % 2, 0:w]).then_inc(s_catTc, 1)
            for n, (c0, w) in enumerate(NCOL):
                dve.wait_ge(s_act0, n + 1)
                ins = V.bn_stats(bnst[:, n, :], actT[:, c0:min(c0 + w, NODES)])
            link(ins)
            link(V.bn_aggr(bnagg[:, 0:2], bnst[:, :, :]))
            V.tensor_scalar(bnagg[:, 2:3], bnagg[:, 1:2], EPS, None, ALU.add).then_inc(s_var, 1)
            std()
            link(V.reciprocal(bnagg[:, 4:5], bnagg[:, 3:4]))
            link(V.tensor_tensor(bnagg[:, 4:5], bnagg[:, 4:5], gamma[:, :], ALU.mult))
            link(V.tensor_tensor(bnagg[:, 5:6], bnagg[:, 0:1], bnagg[:, 4:5], ALU.mult))
            link(V.tensor_tensor(bnagg[:, 5:6], beta[:, :], bnagg[:, 5:6], ALU.subtract))
            V.tensor_scalar(normT, actT, bnagg[:, 4:5], bnagg[:, 5:6], ALU.mult, ALU.add).then_inc(s_norm, 1)
            dve.wait_ge(s_out0, 1)
            for a0, a1, bank in ((0, A_LO, 4), (A_LO, NA, 5)):
                ins = V.tensor_tensor(x[:, a0:a1, :], x[:, a0:a1, :],
                                      ps[:, bank, 0:(a1 - a0) * 32].rearrange("p (a f) -> p a f", f=32), ALU.add)
            link(ins)
            layernorm()
            dve.wait_ge(s_zeroed, 16 * (2 * ZERO_PIECES + 2))
            link(V.memset(table, 0.0))
            rows = table.rearrange("p a (t c) -> p a t c", c=16)
            comps = h[:, :, 8:32].rearrange("p a (v i) -> p a i v", i=3)
            V.tensor_copy(rows[:, :, 0, 0:8], h[:, :, 0:8])
            V.tensor_copy(rows[:, :, 1:4, 0:8], comps)
            V.tensor_copy(rows[:, :, 4:6, 0:8], comps[:, :, 0:2, :]).then_inc(s_table, 1)

            def phase1(s, q, t):
                dve.wait_ge(s_gath[q], 64 * (t + 1))
                F = gath[:, q, :, :].rearrange("p k (t c) -> p k t c", c=16)
                r3 = rdir[:, ds(4 * s, 4), :]
                V.tensor_tensor(cross1[:, :, :, :], r3[:, :, 1:4].unsqueeze(3).broadcast_to([P, 4, 3, 8]),
                                F[:, :, 3:6, 0:8], ALU.mult)
                V.tensor_tensor(cross2[:, :, :, :], r3[:, :, 2:5].unsqueeze(3).broadcast_to([P, 4, 3, 8]),
                                F[:, :, 2:5, 0:8], ALU.mult).then_inc(s_cross, 1)
                V.tensor_tensor(dots[:, :, :, :].rearrange("p k v i -> p k i v"), F[:, :, 1:4, 0:8],
                                r3[:, :, 0:3].unsqueeze(3).broadcast_to([P, 4, 3, 8]), ALU.mult).then_inc(s_cross, 1)
                dve.wait_ge(s_cross, 2 * s + 1)
                V.tensor_tensor(F[:, :, 1:4, 8:16], cross1[:, :, :, :], cross2[:, :, :, :], ALU.subtract)
                dve.wait_ge(s_cross, 2 * s + 2)
                V.tensor_reduce(F[:, :, 0, 8:16], dots[:, :, :, :], AX, ALU.add).then_inc(s_vec, 1)
                mark_earlier(s + STEPS, q)
                dve.wait_ge(s_vec, s + 1)
                for g in range(2):
                    dve.wait_ge(s_rad, 2 * s + g + 1)
                    T = terms[:, g, :, :]
                    V.tensor_tensor(T[:, :, 0:256].rearrange("p k (o x) -> p k o x", o=16),
                                    ps[:, 4 + 2 * g:6 + 2 * g, 0:256].rearrange("p k (o x) -> p k o x", o=16),
                                    F[:, 2 * g:2 * g + 2, 0, :].unsqueeze(2).broadcast_to([P, 2, 16, 16]), ALU.mult)
                    for k in range(2):
                        ins = V.tensor_tensor(
                            T[:, k, 256:640].rearrange("p (u i x) -> p u i x", u=8, i=3),
                            ps[:, 4 + 2 * g + k, 256:384].rearrange("p (u x) -> p u x", u=8)
                            .unsqueeze(2).broadcast_to([P, 8, 3, 16]),
                            F[:, 2 * g + k, 1:4, :].unsqueeze(1).broadcast_to([P, 8, 3, 16]), ALU.mult)
                    ins.then_inc(s_terms, 1)
                if not first(s):
                    dve.wait_ge(s_prod[1], 4 * (s - 1))
                for g in range(2):
                    dve.wait_ge(s_terms, 2 * s + g + 1)
                    V.tensor_reduce(res[:, q, 2 * g:2 * g + 2, 0:40],
                                    terms[:, g, :, :].rearrange("p k (o x) -> p k o x", x=16), AX,
                                    ALU.add).then_inc(s_red, 1)
                entries(s + STEPS, q)
                dve.wait_ge(s_red, 2 * s + 2)
                V.tensor_tensor(along[:, :, :, :], res[:, q, :, 0:8].unsqueeze(3).broadcast_to([P, 4, 8, 3]),
                                r3[:, :, 0:3].unsqueeze(2).broadcast_to([P, 4, 8, 3]), ALU.mult).then_inc(s_along, 1)
                entry_places(s + STEPS)
                dve.wait_ge(s_along, s + 1)
                V.tensor_tensor(res[:, q, :, 16:40], res[:, q, :, 16:40],
                                along[:, :, :, :].rearrange("p k u i -> p k (u i)"), ALU.add).then_inc(s_msg, 1)
                dve.wait_ge(s_msg, s + 1)
                dve.wait_ge(s_wcol, s + 1)
                for k in range(4):
                    products(1, s, q, k, a_dst, res[:, q, k, 8:42], MSG)

            steps(dve, phase1)

            dve.wait_ge(s_sum[1], CH)
            for half in range(2):
                rows_of = len(range(half, NA, 2))
                acc = ps[:, half, 0:rows_of * MSG].rearrange("p (a m) -> p a m", m=MSG)
                V.tensor_tensor(x[:, half:NA:2, :], x[:, half:NA:2, :], acc[:, :, 0:32], ALU.add)
                ins = V.tensor_copy(deg[:, half:NA:2, :], acc[:, :, 32:34])
            link(ins)
            layernorm()
            V.tensor_scalar(dinv[:, 0, :], deg[:, :, 0], 1.2e-35, None, ALU.max)
            V.tensor_scalar(dinv[:, 1, :], deg[:, :, 1], 1.0, None, ALU.add).then_inc(s_var, 1)
            std()
            link(V.reciprocal(dinv[:, :, :], dinv[:, :, :]))
            link(V.scalar_tensor_tensor(out=dinv[:, 0, :], in0=deg[:, :, 0], scalar=0.0, in1=dinv[:, 0, :],
                                        op0=ALU.is_gt, op1=ALU.mult))
            link(V.tensor_tensor(dinv[:, 1, :], dinv[:, 1, :], valid[:, :], ALU.mult))
            turned = ((0, 16, 7), (16, NA, 0))

            def part(a0, a1, bank):
                return ps[:, bank, 0:(a1 - a0) * FEAT].rearrange("p (a f) -> p a f", f=FEAT)

            def copy_sums(r):
                dve.wait_ge(s_mm, NA * (r + 1))
                V.tensor_copy(aggT[:, 0:1536], ps[:, 0:3, :].rearrange("p b n -> p (b n)")).then_inc(s_aggc, 1)
                dve.wait_ge(s_turn, r + 1)

            V.tensor_tensor(zn[:, :, :], h[:, :, :], over_f(dinv[:, 0, :]), ALU.mult).then_inc(s_z, 1)
            link(V.tensor_scalar(cen[:, :, :], h[:, :, :], 1.0 - ALPHA, None, ALU.mult))
            for r in range(3):
                copy_sums(r)
                for a0, a1, bank in turned:
                    ins = V.tensor_tensor(sq[:, a0:a1, :], part(a0, a1, bank),
                                          dinv[:, 0, a0:a1].unsqueeze(2).broadcast_to([P, a1 - a0, FEAT]), ALU.mult)
                link(ins)
                link(V.scalar_tensor_tensor(out=h[:, :, :], in0=sq[:, :, :], scalar=ALPHA, in1=cen[:, :, :],
                                            op0=ALU.mult, op1=ALU.add))
                link(V.tensor_scalar(h[:, :, :], h[:, :, :], 0.0, 1.0, ALU.max, ALU.min))
                if r < 2:
                    V.tensor_tensor(zn[:, :, :], h[:, :, :], over_f(dinv[:, 0, :]), ALU.mult).then_inc(s_z, 1)
            link(V.tensor_tensor(x[:, :, :], x[:, :, :], h[:, :, :], ALU.add))
            layernorm()
            V.tensor_tensor(zn[:, :, :], h[:, :, :], over_f(dinv[:, 1, :]), ALU.mult).then_inc(s_z, 1)

            def over_nodes(i, r, src):
                V.tensor_reduce(fsum[:, 0, :], src.rearrange("p a f -> p f a"), AX, ALU.add).then_inc(s_fs, 1)
                dve.wait_ge(s_fsp, 2 * (r - 3) + i + 1)
                return ps[:, 1, i * FEAT:(i + 1) * FEAT]

            for r in range(3, 6):
                copy_sums(r)
                for a0, a1, bank in turned:
                    ins = V.tensor_tensor(sq[:, a0:a1, :], part(a0, a1, bank), zn[:, a0:a1, :], ALU.add)
                link(ins)
                link(V.tensor_tensor(sq[:, :, :], sq[:, :, :], over_f(dinv[:, 1, :]), ALU.mult))
                link(V.tensor_scalar(h[:, :, :], sq[:, :, :], 0.0, None, ALU.max))
                link(V.tensor_scalar(fsum[:, 1, :], over_nodes(0, r, h[:, :, :]), 1.0 / NODES, None, ALU.mult))
                link(V.tensor_tensor(cen[:, :, :], h[:, :, :], over_a(fsum[:, 1, :]), ALU.subtract))
                link(V.tensor_tensor(cen[:, :, :], cen[:, :, :], over_f(valid[:, :]), ALU.mult))
                link(V.tensor_tensor(sq[:, :, :], cen[:, :, :], cen[:, :, :], ALU.mult))
                V.tensor_scalar(fsum[:, 2, :], over_nodes(1, r, sq[:, :, :]), 1.0 / NODES, EPS,
                                ALU.mult, ALU.add).then_inc(s_var, 1)
                std()
                link(V.reciprocal(fsum[:, 4, :], fsum[:, 3, :]))
                link(V.tensor_tensor(fsum[:, 4, :], fsum[:, 4, :], gam3[:, r - 3, :], ALU.mult))
                link(V.tensor_tensor(sq[:, :, :], cen[:, :, :], over_a(fsum[:, 4, :]), ALU.mult))
                link(V.tensor_tensor(h[:, :, :], sq[:, :, :], over_a(bet3[:, r - 3, :]), ALU.add))
                if r < 5:
                    V.tensor_tensor(zn[:, :, :], h[:, :, :], over_f(dinv[:, 1, :]), ALU.mult).then_inc(s_z, 1)
            V.tensor_tensor(x[:, :, :], x[:, :, :], h[:, :, :], ALU.add).then_inc(s_fin, 1)


_INS = [("x", (NP, FEAT)), ("src", (P, CH)), ("dst", (P, CH)), ("srcT", (112, 7 * P)), ("dstT", (112, 7 * P)),
        ("ea3", (P, CH * 3)), ("ea32", (P, CH * FEAT)), ("w", (P, CH)), ("wT", (CH, P)), ("w1T", (64, HID0)),
        ("b1", (HID0, 1)), ("gamma", (HID0, 1)), ("beta", (HID0, 1)), ("w2T", (HID0, FEAT)), ("b2", (1, FEAT)),
        ("l1w1", (HID1, 1)), ("l1b1", (HID1, 1)), ("l1w2", (HID1, 384)), ("l1b2", (1, 384)),
        ("gam3", (1, 3 * FEAT)), ("bet3", (1, 3 * FEAT))]


def kernel(**inputs):
    import numpy as _np
    import concourse.bacc as _bacc
    from concourse.bass_utils import run_bass_kernel_spmd as _run

    i = {k: _np.asarray(v) for k, v in inputs.items()}

    def padded(a, rows, fill):
        return _np.concatenate([a, _np.full((rows - a.shape[0],) + a.shape[1:], fill, a.dtype)])

    src, dst = (padded(i[k], CH * P, NP - 1).reshape(P, CH) for k in ("src", "dst"))
    w = padded(i["edge_weight"], CH * P, 0).reshape(P, CH)
    data = {
        "x": padded(i["x"], NP, 0), "src": src, "dst": dst,
        "srcT": src.T.reshape(112, 7 * P), "dstT": dst.T.reshape(112, 7 * P),
        "ea3": padded(i["edge_attr_3"], CH * P, 1).reshape(P, CH * 3),
        "ea32": padded(i["edge_attr_32"], CH * P, 0).reshape(P, CH * FEAT),
        "w": w, "wT": w.T,
        "w1T": i["L0_gnn_W1"].T, "b1": i["L0_gnn_b1"], "gamma": i["L0_gnn_gamma"], "beta": i["L0_gnn_beta"],
        "w2T": i["L0_gnn_W2"].T, "b2": i["L0_gnn_b2"],
        "l1w1": i["L1_gnn_w1"], "l1b1": i["L1_gnn_b1"], "l1w2": i["L1_gnn_w2"], "l1b2": i["L1_gnn_b2"],
        "gam3": i["L3_gnn_gammas"], "bet3": i["L3_gnn_betas"],
    }
    nc = _bacc.Bacc("TRN2", target_bir_lowering=False, num_devices=1)
    arrays, args = {}, []
    for name, shape in _INS:
        a = _np.ascontiguousarray(data[name].reshape(shape))
        arrays[f"in_{name}"] = a
        args.append(nc.dram_tensor(f"in_{name}", shape, mybir.dt.from_np(a.dtype), kind="ExternalInput").ap())
    args.append(nc.dram_tensor("out_0", (NODES, FEAT), F32, kind="ExternalOutput").ap())
    gnn_program(nc, *args)
    r = _run(nc, [arrays], core_ids=[0])
    return r.results[0]["out_0"]
```

```python
from contextlib import ExitStack
from math import sqrt

import concourse.bass as bass
from concourse import mybir

ALU = mybir.AluOpType
ACT = mybir.ActivationFunctionType
F32 = mybir.dt.float32
BF16 = mybir.dt.bfloat16
I32 = mybir.dt.int32
AX = mybir.AxisListType.X

P = 128
NODES, EDGES, FEAT = 3125, 100000, 32
NA = -(-NODES // P)
NP = NA * P
LAST = NODES - (NA - 1) * P
CH = -(-EDGES // (16 * P)) * 16
STEPS = CH // 4
PAIRS = CH // 2
PARTS = (2, 4)
HI = [-(-NA // n) for n in PARTS]
A_LO = 13
KEPT = 9
RING = NA - KEPT
HID0, HID1 = 128, 64
MSG = 34
ROW = 96
ZERO_PIECES = 20
BEHIND = 3
FULL = 28
TOGETHER = STEPS - BEHIND + 4 * FULL
EARLY = TOGETHER + 3 * (STEPS // 4 - FULL)
NCOL = [(n, min(512, NP - n)) for n in range(0, NP, 512)]
EPS = 1e-5
ALPHA = 0.9
BIG = NP * NP


def ds(start, size):
    if isinstance(start, int):
        return slice(start, start + size)
    return bass.ds(start, size)


def gnn_program(nc, x_in, src_in, dst_in, srcT_in, dstT_in, ea3_in, ea32_in, ew_in, ewT_in,
                w1T_in, b1_in, gamma_in, beta_in, w2T_in, b2_in, l1w1_in, l1b1_in, l1w2_in, l1b2_in,
                gam3_in, bet3_in, out):
    with ExitStack() as ctx:
        def sb(name, shape, dt=F32):
            return ctx.enter_context(nc.sbuf_tensor(name, shape, dt))

        def sem(name):
            return ctx.enter_context(nc.semaphore(name))

        adj_w = nc.dram_tensor("adj_w", [BIG + 2 * P, 1], F32, kind="Internal").ap()
        adj_c = nc.dram_tensor("adj_c", [BIG + 2 * P, 1], F32, kind="Internal").ap()
        keys_dram = nc.dram_tensor("keys_dram", [CH, P], F32, kind="Internal").ap()
        feat_dram = nc.dram_tensor("feat_dram", [NP, ROW], F32, kind="Internal").ap()

        ident = sb("ident", [P, P])
        stack_id = sb("stack_id", [P, 32])
        iota_b = sb("iota_b", [P, PARTS[1] * P])
        iota_a = sb("iota_a", [P, HI[0]])
        earlier = sb("earlier", [P, P], BF16)
        spare = sb("spare", [P, 2])
        ones_bf = sb("ones_bf", [P, 1], BF16)
        ones_f = sb("ones_f", [P, P])
        zero_bf = sb("zero_bf", [P, 512], BF16)
        valid = sb("valid", [P, NA])

        kept = sb("kept", [P, KEPT, NP])
        kept_all = kept[:, :, :].rearrange("p k n -> p (k n)")
        placed = [0]

        def edge(*dims, dt=F32, parts=P):
            n = 1
            for d in dims:
                n *= d
            words = n // 2 if dt == BF16 else n
            lo = placed[0]
            placed[0] += words
            assert placed[0] <= KEPT * NP
            v = kept_all[0:parts, lo:lo + words]
            if dt != F32:
                v = v.bitcast(dt)
            if len(dims) == 1:
                return v
            names = ["d%d" % i for i in range(len(dims))]
            return v.rearrange("p (%s) -> p %s" % (" ".join(names), " ".join(names)), **dict(zip(names, dims)))

        src_i = edge(CH, dt=I32)
        dst_i = edge(CH, dt=I32)
        key = edge(CH)
        to_spare = edge(CH)
        a_src = edge(CH)
        b_src = edge(CH)
        a_dst = edge(CH)
        b_dst = edge(CH)
        wt = edge(CH)
        wparts = edge(CH, 7, dt=BF16)
        rdir = edge(CH, 5)
        sc_idx = edge(CH)
        sc_val = edge(PAIRS, 2, 2)
        add_to = sb("add_to", [P, 2, 2], I32)
        add_val = sb("add_val", [P, 2, 2, 2])
        count_to = sb("count_to", [P, 2], I32)
        count_val = sb("count_val", [P, 2])
        late_idx = sb("late_idx", [P, 2 * (PAIRS - EARLY)])
        late_val = sb("late_val", [P, PAIRS - EARLY, 2])
        pause = sb("pause", [1, 4])
        take_from = sb("take_from", [P, 2, 4], I32)

        keyrow = edge(2, 2 * P)
        key_gap = edge(2, 2 * P)
        same = edge(2, 2, 2 * P, dt=BF16)
        same_tri = edge(2, 2, P, dt=BF16)
        offs = sb("offs", [P, 2])
        attr = sb("attr", [P, 2, 4, FEAT])
        prod = sb("prod", [P, 2, 4, 448])
        wrow = edge(2, 4 * P, parts=HID1)
        hidT = edge(2, 4 * P, parts=HID1 + 1)
        gath = edge(2, 4, ROW)
        cross1 = edge(4, 3, 8)
        cross2 = edge(4, 3, 8)
        dots = edge(4, 8, 3)
        terms = edge(2, 2, 40 * 16)
        res = edge(2, 4, 42)
        along = edge(4, 8, 3)

        w1T = sb("w1T", [64, HID0])
        b1 = sb("b1", [HID0, 1])
        gamma = sb("gamma", [HID0, 1])
        beta = sb("beta", [HID0, 1])
        w2T = sb("w2T", [HID0, FEAT])
        b2b = sb("b2b", [P, FEAT])
        l1w1 = sb("l1w1", [HID1, 1])
        l1b1 = sb("l1b1", [HID1, 1])
        w2raw = sb("w2raw", [HID1 + 1, 384])
        w2mix = sb("w2mix", [HID1 + 1, 384])
        gam3 = sb("gam3", [P, 3, FEAT])
        bet3 = sb("bet3", [P, 3, FEAT])

        x = sb("x", [P, NA, FEAT])
        h = sb("h", [P, NA, FEAT])
        zn = sb("zn", [P, NA, FEAT])
        cen = sb("cen", [P, NA, FEAT])
        sq = sb("sq", [P, NA, FEAT])
        st = sb("st", [P, 4, NA])
        deg = sb("deg", [P, NA, 2])
        dinv = sb("dinv", [P, 2, NA])
        fsum = sb("fsum", [P, 6, FEAT])
        bnst = sb("bnst", [P, len(NCOL), 6])
        bnagg = sb("bnagg", [P, 6])
        zring = sb("zring", [P, 8, FEAT])

        big = sb("big", [P, 4, NP])
        zeros = big[:, 0, :]
        table = big[:, 0, 0:NA * ROW].rearrange("p (a r) -> p a r", a=NA)
        cat = big[:, 1, 0:NA * 64].rearrange("p (a r) -> p a r", a=NA)
        catT = big[0:64, 2, :]
        actT = big[:, 3, :]
        rel = big[:, 1, 0:CH * 3].rearrange("p (c i) -> p c i", i=3)
        rlen = big[:, 3, 2 * CH:3 * CH]
        rinv = big[:, 3, 3 * CH:4 * CH]
        rings = big[:, 1:3, :].rearrange("p s n -> p (s n)")
        dist2 = rings[:, 0:4 * 512].rearrange("p (k n) -> p k n", k=4)
        onehot = rings[:, 4 * 512:12 * 512].rearrange("p (q k n) -> p q k n", q=2, k=4)
        rel2 = big[:, 2, 0:CH * 3].rearrange("p (c i) -> p c i", i=3)
        tmp_i = big[:, 3, 0:CH].bitcast(I32)
        wrest = big[:, 3, CH:2 * CH]
        prod_all = prod[:, :, :, :].rearrange("p q k n -> p (q k n)")
        srcT = prod_all[0:112, 0:7 * P].bitcast(I32)
        dstT = prod_all[0:112, 7 * P:14 * P].bitcast(I32)
        keyT = prod_all[0:112, 14 * P:21 * P]
        normT = big[:, 1, :]
        aggT = prod_all[:, 0:NP]

        ps = ctx.enter_context(nc.psum_tensor("ps", [P, 8, 512], F32))

        s_in = {n: sem("in_" + n) for n in ("idx", "idxT", "rel", "w", "x", "wts")}
        s_const = sem("const")
        s_zero = sem("zeros_set")
        s_zeroed = sem("adj_zeroed")
        s_keyT = sem("keyT_ready")
        s_keysd = sem("keys_in_dram")
        s_dve = sem("dve_chain")
        s_edge = sem("edge_data_ready")
        s_rlen2 = sem("rel_sq_ready")
        s_rlen = sem("rel_len_ready")
        s_krow = [sem(f"keyrow{q}") for q in range(2)]
        s_attr = [sem(f"attr{q}") for q in range(2)]
        s_wrow = [sem(f"wrow{q}") for q in range(2)]
        s_gath = [sem(f"gath{q}") for q in range(2)]
        s_gap = sem("key_gap_ready")
        s_same = sem("same_ready")
        s_tri = sem("same_tri_ready")
        s_ded = sem("merged_ready")
        s_offs = sem("offs_ready")
        s_idx = sem("scatter_rows_ready")
        s_addto = sem("add_rows_placed")
        s_addval = sem("add_values_placed")
        s_cntto = sem("count_rows_placed")
        s_cntval = sem("count_values_placed")
        s_late = sem("late_counts_kept")
        s_take = sem("gather_rows_placed")
        s_aw = sem("adj_w_added")
        s_ac = sem("adj_c_added")
        s_dist = [sem(f"p{n}_dist_ready") for n in range(2)]
        s_oh = [sem(f"p{n}_onehot_ready") for n in range(2)]
        s_prod = [sem(f"p{n}_prod_ready") for n in range(2)]
        s_sum = [sem(f"p{n}_chunk_summed") for n in range(2)]
        s_open = sem("acc_open")
        s_hid = sem("hidden_ready")
        s_rad = sem("radial_ready")
        s_radfree = sem("radial_used")
        s_cross = sem("cross_terms_ready")
        s_vec = sem("vectors_ready")
        s_terms = sem("terms_ready")
        s_red = sem("terms_summed")
        s_along = sem("along_ready")
        s_msg = sem("messages_ready")
        s_wcol = sem("weight_column_ready")
        s_var = sem("var_ready")
        s_std = sem("std_ready")
        s_cat = sem("cat_ready")
        s_catT = sem("catT_in_psum")
        s_catTc = sem("catT_copied")
        s_h0 = sem("hidden0_in_psum")
        s_act0 = sem("act0_ready")
        s_norm = sem("norm0_ready")
        s_out0 = sem("out0_in_psum")
        s_w2 = sem("w2mix_ready")
        s_table = sem("table_ready")
        s_feat = sem("feat_in_dram")
        s_z = sem("z_ready")
        s_zr = sem("zring_ready")
        s_blk = [sem(f"adj_block{q}") for q in range(4)]
        s_kept = sem("kept_blocks")
        s_mm = sem("block_used")
        s_aggc = sem("agg_copied")
        s_agga = sem("agg_copied_act")
        s_turn = sem("agg_turned")
        s_fs = sem("feature_sums")
        s_fsp = sem("feature_sums_in_psum")
        s_fin = sem("result_ready")
        s_out = sem("out_stored")

        def steps(eng, body):
            for s in range(2):
                body(s, s, 0)
            with eng.Fori(1, STEPS // 2 - 1) as t:
                for q in range(2):
                    body(t * 2 + q, q, t)
            for s in range(STEPS - 2, STEPS):
                body(s, s % 2, s // 2)

        def first(s, n=2):
            return isinstance(s, int) and s < n

        def is_last(s, n=1):
            return isinstance(s, int) and s >= STEPS - n

        def part_sums(n, part, width, rows=None):
            per_bank = PARTS[n] // 2
            c0 = part % per_bank * HI[n] * width
            return ps[:, part // per_bank, c0:c0 + (HI[n] if rows is None else rows) * width]

        block = ctx.enter_context(nc.Block())

        @block.sync
        def _(sp):
            sp.dma_start(srcT, srcT_in).then_inc(s_in["idxT"], 16)
            sp.dma_start(dstT, dstT_in).then_inc(s_in["idxT"], 16)
            sp.dma_start(src_i[:, :], src_in).then_inc(s_in["idx"], 16)
            sp.dma_start(dst_i[:, :], dst_in).then_inc(s_in["idx"], 16)
            sp.dma_start(wt[:, :], ew_in).then_inc(s_in["w"], 16)
            sp.dma_start(x[:, :, :], x_in.rearrange("(a b) f -> b a f", b=P)).then_inc(s_in["x"], 16)
            sp.dma_start(rel[:, :, :], ea3_in).then_inc(s_in["rel"], 16)
            loads = [(w1T[:, :], w1T_in), (b1[:, :], b1_in), (gamma[:, :], gamma_in), (beta[:, :], beta_in),
                     (w2T[:, :], w2T_in), (b2b[:, :], b2_in.broadcast_to([P, FEAT])),
                     (l1w1[:, :], l1w1_in), (l1b1[:, :], l1b1_in),
                     (w2raw[0:HID1, :], l1w2_in), (w2raw[HID1:HID1 + 1, :], l1b2_in),
                     (gam3[:, :, :], gam3_in.broadcast_to([P, 3 * FEAT]).rearrange("p (l f) -> p l f", l=3)),
                     (bet3[:, :, :], bet3_in.broadcast_to([P, 3 * FEAT]).rearrange("p (l f) -> p l f", l=3))]
            for dst, src in loads:
                sp.dma_start(dst, src).then_inc(s_in["wts"], 16)

            sp.wait_ge(s_keyT, 1)
            sp.dma_start(keys_dram.rearrange("(q j) p -> q (j p)", j=7), keyT).then_inc(s_keysd, 16)
            sp.wait_ge(s_keysd, 16)

            def load_keys(d, q):
                if not first(d):
                    sp.wait_ge(s_gap, 2 * (d - 1))
                row = keys_dram[ds(2 * d, 2), :].rearrange("(o c) p -> o (c p)", o=1)
                sp.dma_start(keyrow[:, q, :], row.broadcast_to([P, 2 * P])).then_inc(s_krow[q], 16)

            def load0(s, q, t):
                load_keys(s, q)
                if not first(s):
                    sp.wait_ge(s_prod[0], 4 * (s - 1))
                sp.dma_start(attr[:, q, :, :].rearrange("p k f -> p (k f)"),
                             ea32_in[:, ds(s * (4 * FEAT), 4 * FEAT)]).then_inc(s_attr[q], 16)

            steps(sp, load0)
            sp.wait_ge(s_table, 1)
            sp.dma_start(feat_dram.rearrange("(a b) r -> b a r", b=P), table).then_inc(s_feat, 16)

            def load1(s, q, t):
                load_keys(s + STEPS, q)
                if not first(s):
                    sp.wait_ge(s_hid, s - 1)
                row = ewT_in[ds(4 * s, 4), :].rearrange("(o c) p -> o (c p)", o=1)
                sp.dma_start(wrow[:, q, :], row.broadcast_to([HID1, 4 * P])).then_inc(s_wrow[q], 16)

            steps(sp, load1)

            sp.wait_ge(s_aw, 32 * PAIRS)
            sp.wait_ge(s_ac, 32 * EARLY)
            sp.wait_ge(s_late, 1)
            sp.wait_ge(s_feat, 16)
            sp.wait_ge(s_sum[1], CH)

            def load_round(r, adj):
                for i in range(RING):
                    if i >= 12:
                        sp.wait_ge(s_mm, r * NA + (i + KEPT - 3))
                    elif i >= 4 or not first(r, 1):
                        sp.wait_ge(s_mm, r * NA + (i - 3))
                    m = i if i < RING // 2 else i + KEPT
                    sp.dma_start(big[:, i % 4, :], adj[m * P:(m + 1) * P, :]).then_inc(s_blk[i % 4], 16)

            for layer, sums in enumerate((adj_w, adj_c)):
                adj = sums[0:BIG, :].rearrange("(s d) o -> s (d o)", d=NP)
                if layer == 1:
                    sp.wait_ge(s_ac, 32 * PAIRS)
                    sp.wait_ge(s_mm, 2 * NA + RING // 2 + KEPT)
                for c in range(KEPT):
                    m = RING // 2 + c
                    sp.dma_start(kept[:, c, :], adj[m * P:(m + 1) * P, :]).then_inc(s_kept, 16)
                load_round(3 * layer, adj)
                with sp.Fori(3 * layer + 1, 3 * layer + 3) as r:
                    load_round(r, adj)

            sp.wait_ge(s_fin, 1)
            sp.dma_start(out[0:(NA - 1) * P, :].rearrange("(a b) f -> b a f", b=P),
                         x[:, 0:NA - 1, :]).then_inc(s_out, 16)
            sp.dma_start(out[(NA - 1) * P:NODES, :], x[0:LAST, NA - 1, :]).then_inc(s_out, 16)
            sp.wait_ge(s_out, 32)

        @block.gpsimd
        def _(pool):
            pool.memset(zeros, 0.0).then_inc(s_zero, 1)
            pool.memset(ident[:, :], 0.0).then_inc(s_const, 1)
            pool.memset(earlier[:, :], 1.0).then_inc(s_const, 1)
            pool.memset(valid[:, :], 1.0).then_inc(s_const, 1)
            pool.wait_ge(s_const, 3)
            pool.affine_select(out=ident[:, :], in_=ident[:, :], compare_op=ALU.not_equal, fill=1.0,
                               base=0, pattern=[[-1, P]], channel_multiplier=1).then_inc(s_const, 1)
            pool.affine_select(out=earlier[:, :], in_=earlier[:, :], compare_op=ALU.is_gt, fill=0.0,
                               base=0, pattern=[[1, P]], channel_multiplier=-1).then_inc(s_const, 1)
            pool.affine_select(out=valid[:, :], in_=valid[:, :], compare_op=ALU.is_gt, fill=0.0,
                               base=NODES, pattern=[[-P, NA]], channel_multiplier=-1).then_inc(s_const, 1)
            pool.iota(iota_b[:, :], [[1, PARTS[1] * P]], base=0, channel_multiplier=0,
                      allow_small_or_imprecise_dtypes=True).then_inc(s_const, 1)
            pool.iota(iota_a[:, :], [[1, HI[0]]], base=0, channel_multiplier=0,
                      allow_small_or_imprecise_dtypes=True).then_inc(s_const, 1)
            pool.iota(spare[:, :], [[P, 2]], base=BIG, channel_multiplier=1,
                      allow_small_or_imprecise_dtypes=True).then_inc(s_const, 1)

            last_entry = pool.to_reg(BIG + 2 * P - 1)
            last_node = pool.to_reg(NP - 1)

            def snap(v):
                return v if isinstance(v, int) else pool.snap(v)

            def hold_for_waits(n):
                pool.tensor_tensor(pause[:, n:n + 1], spare[0:1, 0:1], spare[0:1, 1:2], ALU.add)

            def add_pair(d, q, kinds=(0, 1)):
                ready, landed = snap(d + 1), snap(d * 32)
                idx, val = sc_idx[:, ds(2 * d, 2)], sc_val[:, ds(d, 1), :, :].rearrange("p d v j -> p (d v) j")
                pool.wait_ge(s_idx, ready)
                pool.tensor_copy(add_to[:, q, :], idx).then_inc(s_addto, 1)
                pool.tensor_copy(add_val[:, q, :, :], val).then_inc(s_addval, 1)
                pool.wait_ge(s_addto, ready)
                pool.wait_ge(s_addval, ready)
                for v in kinds:
                    adj, done = ((adj_c, s_ac), (adj_w, s_aw))[v]
                    if not first(d, 1):
                        pool.wait_ge(done, landed)
                    hold_for_waits(v)
                    for j in range(2):
                        pool.indirect_dma_start(adj, bass.IndirectOffsetOnAxis(ap=add_to[:, q, j:j + 1], axis=0),
                                                add_val[:, q, v, j:j + 1], None, bounds_check=last_entry,
                                                compute_op=ALU.add).then_inc(done, 16)

            def add_counts(d, idx, val):
                n = d - TOGETHER
                placed, landed = snap(n + 1), snap(d * 32)
                pool.wait_ge(s_ac, landed)
                pool.tensor_copy(count_to[:, :], idx).then_inc(s_cntto, 1)
                pool.tensor_copy(count_val[:, :], val).then_inc(s_cntval, 1)
                pool.wait_ge(s_cntto, placed)
                pool.wait_ge(s_cntval, placed)
                hold_for_waits(3)
                for j in range(2):
                    pool.indirect_dma_start(adj_c, bass.IndirectOffsetOnAxis(ap=count_to[:, j:j + 1], axis=0),
                                            count_val[:, j:j + 1], None, bounds_check=last_entry,
                                            compute_op=ALU.add).then_inc(s_ac, 16)

            pool.wait_ge(s_zeroed, 16 * (2 * ZERO_PIECES + 2))

            add_pair(0, 0)
            with pool.Fori(0, (STEPS - BEHIND - 1) // 2) as t:
                add_pair(t * 2 + 1, 1)
                add_pair(t * 2 + 2, 0)
            pool.wait_ge(s_feat, 16)

            def gather(s, q):
                taken = snap(s + 1)
                if not first(s):
                    pool.wait_ge(s_terms, snap(2 * (s - 1)))
                pool.tensor_copy(take_from[:, q, :], src_i[:, ds(4 * s, 4)]).then_inc(s_take, 1)
                pool.wait_ge(s_take, taken)
                hold_for_waits(2)
                for k in range(4):
                    pool.indirect_dma_start(gath[:, q, k, :], None, feat_dram,
                                            bass.IndirectOffsetOnAxis(ap=take_from[:, q, k:k + 1], axis=0),
                                            bounds_check=last_node).then_inc(s_gath[q], 16)

            gather(0, 0)

            def four_steps(t, counts):
                for k in range(4):
                    s, q = t * 4 + k, k % 2
                    if not is_last(s):
                        gather(s + 1, 1 - q)
                    add_pair(s + (STEPS - BEHIND), 1 - q, (0, 1) if counts == 4 else (1,))
                    if k < counts < 4:
                        c = t * 3 + (STEPS - BEHIND + FULL + k)
                        add_counts(c, sc_idx[:, ds(2 * c, 2)],
                                   sc_val[:, ds(c, 1), 0, :].rearrange("p d j -> p (d j)"))

            four_steps(0, 4)
            with pool.Fori(1, FULL) as t:
                four_steps(t, 4)
            with pool.Fori(FULL, STEPS // 4 - 1) as t:
                four_steps(t, 3)
            four_steps(STEPS // 4 - 1, 3)
            for d in range(PAIRS - BEHIND, PAIRS):
                add_pair(d, d % 2, (1,))
            pool.wait_ge(s_late, 1)
            with pool.Fori(0, PAIRS - EARLY) as i:
                add_counts(i + EARLY, late_idx[:, ds(2 * i, 2)], late_val[:, ds(i, 1), :].rearrange("p d j -> p (d j)"))

        @block.scalar
        def _(act):
            act.wait_ge(s_zero, 1)
            act.wait_ge(s_keysd, 16)
            for adj in (adj_w, adj_c):
                act.dma_start(adj[BIG:BIG + 2 * P, :].rearrange("(p c) o -> p (c o)", p=P),
                              zeros[:, 0:2]).then_inc(s_zeroed, 16)

            def zero_piece(t, adj):
                act.dma_start(adj[ds(t * (BIG // ZERO_PIECES), BIG // ZERO_PIECES), :]
                              .rearrange("(p i c) o -> p i (c o)", p=P, i=2),
                              zeros[:, 0:BIG // ZERO_PIECES // P // 2].unsqueeze(1)
                              .broadcast_to([P, 2, BIG // ZERO_PIECES // P // 2])).then_inc(s_zeroed, 16)

            for t in range(2):
                for adj in (adj_w, adj_c):
                    zero_piece(t, adj)
            ln = [0]

            def std():
                ln[0] += 1
                act.wait_ge(s_var, ln[0])
                act.activation(st[:, 3, :], st[:, 2, :], ACT.Sqrt).then_inc(s_std, 1)

            std()
            act.wait_ge(s_rlen2, 1)
            act.activation(rlen[:, :], rinv[:, :], ACT.Sqrt).then_inc(s_rlen, 1)
            act.wait_ge(s_const, 9)

            def compare(d, q):
                act.wait_ge(s_krow[q], d * 8 - q * 8 + 16)
                if not first(d, 1):
                    act.wait_ge(s_same, d)
                for i in range(2):
                    act.activation(key_gap[:, i, :], keyrow[:, q, :], ACT.Square, scale=-1.0,
                                   bias=key[:, ds(2 * d + i, 1)]).then_inc(s_gap, 1)
                act.wait_ge(s_gap, 2 * d + 2)
                if not first(d):
                    act.wait_ge(s_ded, d - 1)
                act.activation(same[:, q, :, :], key_gap[:, :, :], ACT.Relu, scale=-1.0,
                               bias=1.0).then_inc(s_same, 1)

            def onehots(n, s, q, bcol):
                wide = PARTS[n] * P
                if not first(s, 1):
                    act.wait_ge(s_oh[n], s)
                for k in range(4):
                    act.activation(dist2[:, k, 0:wide], iota_b[:, 0:wide], ACT.Square, scale=-1.0,
                                   bias=bcol[:, ds(4 * s + k, 1)]).then_inc(s_dist[n], 1)
                act.wait_ge(s_dist[n], 4 * (s + 1))
                if not first(s):
                    act.wait_ge(s_sum[n], 4 * (s - 1))
                act.activation(onehot[:, q, :, 0:wide], dist2[:, :, 0:wide], ACT.Relu, scale=-1.0,
                               bias=1.0).then_inc(s_oh[n], 1)

            act.wait_ge(s_edge, 1)

            def phase0(s, q, t):
                compare(s, q)
                onehots(0, s, q, b_src)

            for q in range(2):
                phase0(q, q, 0)
            with act.Fori(1, ZERO_PIECES - 1) as t:
                for q, adj in enumerate((adj_w, adj_c)):
                    zero_piece(t + 1, adj)
                    phase0(t * 2 + q, q, t)
            with act.Fori(ZERO_PIECES - 1, STEPS // 2) as t:
                for q in range(2):
                    phase0(t * 2 + q, q, t)

            for n, (c0, w) in enumerate(NCOL):
                act.wait_ge(s_h0, n + 1)
                act.activation(actT[:, c0:c0 + w], ps[:, 6 + n % 2, 0:w], ACT.Relu,
                               bias=b1[:, 0:1]).then_inc(s_act0, 1)
            act.wait_ge(s_var, 2)
            act.activation(bnagg[:, 3:4], bnagg[:, 2:3], ACT.Sqrt).then_inc(s_std, 1)
            ln[0] += 1
            std()

            def phase1(s, q, t):
                compare(s + STEPS, q)
                act.wait_ge(s_wrow[q], 16 * (t + 1))
                if not first(s):
                    act.wait_ge(s_rad, 2 * (s - 1))
                act.activation(hidT[0:HID1, q, :], wrow[:, q, :], ACT.Relu, scale=l1w1[:, 0:1],
                               bias=l1b1[:, 0:1]).then_inc(s_hid, 1)
                if not first(s):
                    act.wait_ge(s_prod[1], 4 * (s - 1))
                act.activation(res[:, q, :, 40:41], wt[:, ds(4 * s, 4)].unsqueeze(2), ACT.Copy).then_inc(s_wcol, 1)
                onehots(1, s, q, b_dst)

            steps(act, phase1)
            std()
            ln[0] += 1
            act.wait_ge(s_var, ln[0])
            act.activation(dinv[:, :, :], dinv[:, :, :], ACT.Sqrt).then_inc(s_std, 1)

            for r in range(6):
                act.wait_ge(s_z, r + 1)

                def copy_z(i, half):
                    if not first(i, 1):
                        act.wait_ge(s_mm, NA * r + 8 * i + 4 * half - 4)
                    act.activation(zring[:, 4 * half:4 * half + 4, :], zn[:, ds(8 * i + 4 * half, 4), :],
                                   ACT.Copy).then_inc(s_zr, 1)

                copy_z(0, 0)
                copy_z(0, 1)
                with act.Fori(1, NA // 8) as i:
                    copy_z(i, 0)
                    copy_z(i, 1)
                act.wait_ge(s_mm, NA * r + 20)
                act.activation(zring[:, 0:1, :], zn[:, NA - 1:NA, :], ACT.Copy).then_inc(s_zr, 1)
                act.wait_ge(s_mm, NA * (r + 1))
                for n in (1, 3, 5, 6):
                    c0, w = NCOL[n]
                    act.activation(aggT[:, c0:c0 + w], ps[:, n, 0:w], ACT.Copy).then_inc(s_agga, 1)
                if r == 2:
                    std()
                if r >= 3:
                    act.wait_ge(s_var, 4 + r)
                    act.activation(fsum[:, 3, :], fsum[:, 2, :], ACT.Sqrt).then_inc(s_std, 1)

        @block.tensor
        def _(pe):
            def open_banks(banks):
                for n in banks:
                    mm = pe.matmul(ps[:, n, :], zero_bf[:, 0:P], zero_bf[:, :], start=True, stop=True,
                                   skip_group_check=True)
                return mm

            def merge(d, q):
                pe.wait_ge(s_tri, d + 1)
                if not first(d):
                    pe.wait_ge(s_idx, d - 1)
                o = ps[:, 2 + q, 0:14].rearrange("p (j v) -> p j v", j=2)
                for j in range(2):
                    pe.matmul(o[:, j, 0:1], same_tri[:, q, j, :], ones_bf[:, :], start=(j == 0), stop=False,
                              skip_group_check=True)
                    for i in range(2):
                        lo = 0 if (i, j) == (0, 1) else 1
                        mm = pe.matmul(o[:, j, lo:7], same[:, q, i, j * P:(j + 1) * P],
                                       wparts[:, ds(2 * d + i, 1), lo:7].rearrange("p c v -> p (c v)"),
                                       start=False, stop=(i == 1), skip_group_check=True)
                mm.then_inc(s_ded, 1)

            def scatter(n, s, q, k, width):
                pe.wait_ge(s_oh[n], s + 1)
                pe.wait_ge(s_prod[n], 4 * s + k + 1)
                for part in range(PARTS[n]):
                    mm = pe.matmul(part_sums(n, part, width), onehot[:, q, k, part * P:(part + 1) * P],
                                   prod[:, q, k, 0:HI[n] * width], start=False, stop=False, skip_group_check=True)
                mm.then_inc(s_sum[n], 1)

            pe.wait_ge(s_open, 1)
            open_banks(range(2))
            pe.wait_ge(s_edge, 1)

            def phase0(s, q, t):
                merge(s, q)
                for k in range(4):
                    scatter(0, s, q, k, FEAT)

            steps(pe, phase0)

            pe.wait_ge(s_cat, 1)
            for g in range(len(NCOL)):
                if g >= 2:
                    pe.wait_ge(s_catTc, g - 1)
                for a in range(4 * g, min(4 * g + 4, NA)):
                    mm = pe.transpose(ps[0:64, 4 + g % 2, (a % 4) * P:(a % 4 + 1) * P], cat[:, a, :], ident[:, :])
                mm.then_inc(s_catT, 1)
            for n, (c0, w) in enumerate(NCOL):
                pe.wait_ge(s_catTc, n + 1)
                if n >= 2:
                    pe.wait_ge(s_act0, n - 1)
                pe.matmul(ps[:, 6 + n % 2, 0:w], w1T[:, :], catT[:, c0:c0 + w], start=True,
                          stop=True).then_inc(s_h0, 1)
            open_banks(range(2))
            pe.wait_ge(s_norm, 1)
            for a in range(NA):
                bank, col = (4, a) if a < A_LO else (5, a - A_LO)
                mm = pe.matmul(ps[:, bank, col * FEAT:(col + 1) * FEAT], normT[:, a * P:(a + 1) * P], w2T[:, :],
                               start=True, stop=True)
            mm.then_inc(s_out0, 1)

            def radial(s, q, g):
                pe.wait_ge(s_hid, s + 1)
                if not first(s, 1):
                    pe.wait_ge(s_terms, 2 * s - 1 + g)
                for k in (2 * g, 2 * g + 1):
                    mm = pe.matmul(ps[:, 4 + k, 0:384], hidT[:, q, k * P:(k + 1) * P], w2mix[:, :],
                                   start=True, stop=True)
                mm.then_inc(s_rad, 1)

            pe.wait_ge(s_table, 1)
            radial(0, 0, 0)
            radial(0, 0, 1)

            def phase1(s, q, t):
                merge(s + STEPS, q)
                if not is_last(s):
                    for g in range(2):
                        radial(s + 1, 1 - q, g)
                for k in range(4):
                    scatter(1, s, q, k, MSG)

            steps(pe, phase1)

            def spmm_round(r, norm):
                pe.wait_ge(s_z, r + 1)

                def block_times_z(m, values):
                    pe.wait_ge(s_zr, r * 7 + (m // 4 + 1))
                    g = 32 * (m % 4)
                    for n, (c0, w) in enumerate(NCOL):
                        mm = pe.matmul(ps[g:g + 32, n, 0:w], zring[:, m % 8, :], values[:, c0:c0 + w],
                                       start=(m < 4), stop=(m >= NA - 4), skip_group_check=True)
                    mm.then_inc(s_mm, 1)

                def ring_block(i):
                    m = i if i < RING // 2 else i + KEPT
                    pe.wait_ge(s_blk[i % 4], r * (RING // 4 * 16) + (i // 4 + 1) * 16)
                    block_times_z(m, big[:, i % 4, :])

                for i in range(RING // 2):
                    ring_block(i)
                pe.wait_ge(s_kept, 16 * KEPT * (2 if norm else 1))
                for c in range(KEPT):
                    block_times_z(RING // 2 + c, kept[:, c, :])
                for i in range(RING // 2, RING):
                    ring_block(i)
                for a in range(NA):
                    if a in (0, 8, 16):
                        pe.wait_ge(s_aggc, r * 3 + (a // 8 + 1))
                    if a in (4, 12, 20, 24):
                        pe.wait_ge(s_agga, r * 4 + {4: 1, 12: 2, 20: 3, 24: 4}[a])
                    bank, col = (7, a) if a < 16 else (0, a - 16)
                    mm = pe.matmul(ps[:, bank, col * FEAT:(col + 1) * FEAT], aggT[:, a * P:(a + 1) * P],
                                   stack_id[:, :], start=True, stop=True)
                mm.then_inc(s_turn, 1)
                if norm:
                    for i in range(2):
                        pe.wait_ge(s_fs, r * 2 - 6 + i + 1)
                        pe.matmul(ps[:, 1, i * FEAT:(i + 1) * FEAT], ones_f[:, :], fsum[:, 0, :],
                                  start=True, stop=True).then_inc(s_fsp, 1)

            with pe.Fori(0, 3) as r:
                spmm_round(r, False)
            with pe.Fori(3, 6) as r:
                spmm_round(r, True)

        @block.vector
        def _(dve):
            chain = [0]

            def link(ins):
                chain[0] += 1
                ins.then_inc(s_dve, 1)
                dve.wait_ge(s_dve, chain[0])

            def over_f(t):
                return t.unsqueeze(2).broadcast_to([P, NA, FEAT])

            def over_a(t):
                return t.unsqueeze(1).broadcast_to([P, NA, FEAT])

            V = nc.vector
            jobs = [0]

            def std():
                jobs[0] += 1
                dve.wait_ge(s_std, jobs[0])

            def layernorm():
                link(V.tensor_reduce(st[:, 0, :], x[:, :, :], AX, ALU.add))
                link(V.tensor_scalar(st[:, 1, :], st[:, 0, :], 1.0 / FEAT, None, ALU.mult))
                link(V.tensor_tensor(cen[:, :, :], x[:, :, :], over_f(st[:, 1, :]), ALU.subtract))
                link(V.tensor_tensor(sq[:, :, :], cen[:, :, :], cen[:, :, :], ALU.mult))
                link(V.tensor_reduce(st[:, 0, :], sq[:, :, :], AX, ALU.add))
                V.tensor_scalar(st[:, 2, :], st[:, 0, :], 1.0 / FEAT, EPS, ALU.mult, ALU.add).then_inc(s_var, 1)
                std()
                link(V.reciprocal(st[:, 1, :], st[:, 3, :]))
                link(V.tensor_tensor(sq[:, :, :], cen[:, :, :], over_f(st[:, 1, :]), ALU.mult))
                link(V.tensor_scalar(h[:, :, :], sq[:, :, :], 0.0, None, ALU.max))

            V.memset(zero_bf[:, :], 0.0).then_inc(s_open, 1)
            V.memset(ones_bf[:, :], 1.0)
            V.memset(ones_f[:, :], 1.0)
            V.memset(wparts[:, :, 0:2], 1.0)
            V.memset(wparts[:, :, 2:4], 0.0)
            V.memset(res[:, :, :, 41:42], 1.0)
            link(V.memset(hidT[HID1:HID1 + 1, :, :], 1.0))

            dve.wait_ge(s_in["idxT"], 32)
            V.scalar_tensor_tensor(out=keyT, in0=srcT, scalar=float(NP), in1=dstT,
                                   op0=ALU.mult, op1=ALU.add).then_inc(s_keyT, 1)
            dve.wait_ge(s_in["idx"], 32)
            link(V.scalar_tensor_tensor(out=key[:, :], in0=src_i[:, :], scalar=float(NP), in1=dst_i[:, :],
                                        op0=ALU.mult, op1=ALU.add))
            for ids, hi, lo, n in ((src_i, a_src, b_src, 0), (dst_i, a_dst, b_dst, 1)):
                wide = PARTS[n] * P
                link(V.tensor_scalar(tmp_i, ids[:, :], wide.bit_length() - 1, None, ALU.arith_shift_right))
                link(V.tensor_copy(hi[:, :], tmp_i))
                link(V.tensor_scalar(tmp_i, ids[:, :], wide - 1, None, ALU.bitwise_and))
                link(V.tensor_copy(lo[:, :], tmp_i))
            dve.wait_ge(s_const, 9)
            link(V.tensor_tensor(to_spare[:, :].rearrange("p (d j) -> p d j", j=2),
                                 spare[:, :].unsqueeze(1).broadcast_to([P, PAIRS, 2]),
                                 key[:, :].rearrange("p (d j) -> p d j", j=2), ALU.subtract))
            dve.wait_ge(s_in["w"], 16)
            link(V.tensor_copy(wparts[:, :, 4], wt[:, :]))
            link(V.tensor_tensor(wrest, wt[:, :], wparts[:, :, 4], ALU.subtract))
            link(V.tensor_copy(wparts[:, :, 5], wrest))
            link(V.tensor_tensor(wrest, wrest, wparts[:, :, 5], ALU.subtract))
            link(V.tensor_copy(wparts[:, :, 6], wrest))
            link(V.tensor_tensor(stack_id[:, :], ident[:, 0:32], ident[:, 32:64], ALU.add))
            link(V.tensor_tensor(stack_id[:, :], stack_id[:, :], ident[:, 64:96], ALU.add))
            link(V.tensor_tensor(stack_id[:, :], stack_id[:, :], ident[:, 96:128], ALU.add))
            dve.wait_ge(s_in["x"], 16)
            layernorm()
            dve.wait_ge(s_in["rel"], 16)
            link(V.tensor_tensor(rel2[:, :, :], rel[:, :, :], rel[:, :, :], ALU.mult))
            V.tensor_reduce(rinv[:, :], rel2[:, :, :], AX, ALU.add).then_inc(s_rlen2, 1)
            dve.wait_ge(s_rlen, 1)
            link(V.reciprocal(rinv[:, :], rlen[:, :]))
            link(V.tensor_tensor(rdir[:, :, 0:2], rel[:, :, 1:3],
                                 rinv[:, :].unsqueeze(2).broadcast_to([P, CH, 2]), ALU.mult))
            V.tensor_tensor(rdir[:, :, 2:5], rel[:, :, :],
                            rinv[:, :].unsqueeze(2).broadcast_to([P, CH, 3]), ALU.mult).then_inc(s_edge, 1)
            dve.wait_ge(s_edge, 1)

            def mark_earlier(d, q):
                dve.wait_ge(s_same, d + 1)
                if not first(d):
                    dve.wait_ge(s_ded, d - 1)
                within = same[:, q, :, :].rearrange("p i (j e) -> p (i j) e", j=2)[:, 0:4:3, :]
                V.tensor_tensor(same_tri[:, q, :, :], within, earlier[:, :].unsqueeze(1).broadcast_to([P, 2, P]),
                                ALU.mult).then_inc(s_tri, 1)

            def entries(d, q):
                dve.wait_ge(s_ded, d + 1)
                if not first(d, 1):
                    dve.wait_ge(s_idx, d)
                m = ps[:, 2 + q, 0:14].rearrange("p (j v) -> p j v", j=2)
                V.tensor_reduce(sc_val[:, ds(d, 1), :, :].rearrange("p d v j -> p (d j) v"),
                                m[:, :, 1:7].rearrange("p j (v i) -> p j v i", i=3), AX, ALU.add)
                V.scalar_tensor_tensor(out=offs[:, :], in0=m[:, :, 0], scalar=0.0, in1=to_spare[:, ds(2 * d, 2)],
                                       op0=ALU.is_gt, op1=ALU.mult).then_inc(s_offs, 1)

            def entry_places(d):
                dve.wait_ge(s_offs, d + 1)
                V.tensor_tensor(sc_idx[:, ds(2 * d, 2)], offs[:, :], key[:, ds(2 * d, 2)],
                                ALU.add).then_inc(s_idx, 1)

            def products(n, s, q, k, acol, rows, width):
                if not first(s):
                    dve.wait_ge(s_sum[n], 4 * s - 8 + k + 1)
                V.scalar_tensor_tensor(
                    out=prod[:, q, k, 0:HI[n] * width].rearrange("p (a m) -> p a m", a=HI[n]),
                    in0=iota_a[:, 0:HI[n]].unsqueeze(2).broadcast_to([P, HI[n], width]),
                    scalar=acol[:, ds(4 * s + k, 1)], in1=rows.unsqueeze(1).broadcast_to([P, HI[n], width]),
                    op0=ALU.is_equal, op1=ALU.mult).then_inc(s_prod[n], 1)

            def phase0(s, q, t):
                mark_earlier(s, q)
                dve.wait_ge(s_attr[q], 16 * (t + 1))
                for k in range(4):
                    products(0, s, q, k, a_src, attr[:, q, k, :], FEAT)
                    if k == 2:
                        entries(s, q)
                entry_places(s)

            steps(dve, phase0)

            dve.wait_ge(s_in["wts"], 16 * 12)
            dve.wait_ge(s_sum[0], CH)
            V.tensor_copy(cat[:, :, 0:32], h[:, :, :])
            for part in range(PARTS[0]):
                rows = len(range(part, NA, PARTS[0]))
                ins = V.tensor_copy(cat[:, part:NA:PARTS[0], 32:64],
                                    part_sums(0, part, FEAT, rows).rearrange("p (a f) -> p a f", f=FEAT))
            ins.then_inc(s_cat, 1)
            link(V.tensor_tensor(x[:, :, :], x[:, :, :], over_a(b2b[:, :]), ALU.add))
            for g, (c0, w) in enumerate(NCOL):
                dve.wait_ge(s_catT, g + 1)
                V.tensor_copy(catT[:, c0:c0 + w], ps[0:64, 4 + g % 2, 0:w]).then_inc(s_catTc, 1)
            for n, (c0, w) in enumerate(NCOL):
                dve.wait_ge(s_act0, n + 1)
                ins = V.bn_stats(bnst[:, n, :], actT[:, c0:min(c0 + w, NODES)])
            link(ins)
            link(V.bn_aggr(bnagg[:, 0:2], bnst[:, :, :]))
            V.tensor_scalar(bnagg[:, 2:3], bnagg[:, 1:2], EPS, None, ALU.add).then_inc(s_var, 1)
            std()
            link(V.reciprocal(bnagg[:, 4:5], bnagg[:, 3:4]))
            link(V.tensor_tensor(bnagg[:, 4:5], bnagg[:, 4:5], gamma[:, :], ALU.mult))
            link(V.tensor_tensor(bnagg[:, 5:6], bnagg[:, 0:1], bnagg[:, 4:5], ALU.mult))
            link(V.tensor_tensor(bnagg[:, 5:6], beta[:, :], bnagg[:, 5:6], ALU.subtract))
            V.tensor_scalar(normT, actT, bnagg[:, 4:5], bnagg[:, 5:6], ALU.mult, ALU.add).then_inc(s_norm, 1)
            R00, R01, R10 = (w2raw[:, n * 64:(n + 1) * 64].rearrange("h (u v) -> h u v", u=8) for n in range(3))
            R11 = w2raw[:, 192:384].rearrange("h (u v k) -> h u v k", u=8, v=8)
            Q = w2mix[:, 0:256].rearrange("h (o x) -> h o x", o=16)
            AB = w2mix[:, 256:384].rearrange("h (u x) -> h u x", u=8)
            V.tensor_scalar(Q[:, 0:8, 0:8], R10, sqrt(3 / 32), None, ALU.mult)
            V.tensor_scalar(Q[:, 0:8, 8:16], R11[:, :, :, 2], 3 / 8, None, ALU.mult)
            V.tensor_scalar(Q[:, 8:16, 0:8], R00, 0.25, None, ALU.mult)
            V.tensor_scalar(Q[:, 8:16, 8:16], R01, 0.25, None, ALU.mult)
            V.tensor_scalar(AB[:, :, 8:16], R11[:, :, :, 1], sqrt(3) / 8, None, ALU.mult)
            link(V.tensor_scalar(AB[:, :, 0:8], R11[:, :, :, 0], 1 / sqrt(32), None, ALU.mult))
            link(V.scalar_tensor_tensor(out=AB[:, :, 0:8], in0=R11[:, :, :, 2], scalar=-1 / 8, in1=AB[:, :, 0:8],
                                        op0=ALU.mult, op1=ALU.add))

            dve.wait_ge(s_out0, 1)
            for a0, a1, bank in ((0, A_LO, 4), (A_LO, NA, 5)):
                ins = V.tensor_tensor(x[:, a0:a1, :], x[:, a0:a1, :],
                                      ps[:, bank, 0:(a1 - a0) * 32].rearrange("p (a f) -> p a f", f=32), ALU.add)
            link(ins)
            layernorm()
            dve.wait_ge(s_zeroed, 16 * (2 * ZERO_PIECES + 2))
            rows = table.rearrange("p a (t c) -> p a t c", c=16)
            comps = h[:, :, 8:32].rearrange("p a (v i) -> p a i v", i=3)
            V.tensor_copy(rows[:, :, 0, 0:8], h[:, :, 0:8])
            V.tensor_copy(rows[:, :, 1:4, 0:8], comps)
            V.tensor_copy(rows[:, :, 4:6, 0:8], comps[:, :, 0:2, :]).then_inc(s_table, 1)

            def phase1(s, q, t):
                dve.wait_ge(s_gath[q], 64 * (t + 1))
                F = gath[:, q, :, :].rearrange("p k (t c) -> p k t c", c=16)
                r3 = rdir[:, ds(4 * s, 4), :]
                V.tensor_tensor(cross1[:, :, :, :], r3[:, :, 1:4].unsqueeze(3).broadcast_to([P, 4, 3, 8]),
                                F[:, :, 3:6, 0:8], ALU.mult)
                V.tensor_tensor(cross2[:, :, :, :], r3[:, :, 2:5].unsqueeze(3).broadcast_to([P, 4, 3, 8]),
                                F[:, :, 2:5, 0:8], ALU.mult).then_inc(s_cross, 1)
                V.tensor_tensor(dots[:, :, :, :].rearrange("p k v i -> p k i v"), F[:, :, 1:4, 0:8],
                                r3[:, :, 0:3].unsqueeze(3).broadcast_to([P, 4, 3, 8]), ALU.mult).then_inc(s_cross, 1)
                dve.wait_ge(s_cross, 2 * s + 1)
                V.tensor_tensor(F[:, :, 1:4, 8:16], cross1[:, :, :, :], cross2[:, :, :, :], ALU.subtract)
                dve.wait_ge(s_cross, 2 * s + 2)
                V.tensor_reduce(F[:, :, 0, 8:16], dots[:, :, :, :], AX, ALU.add).then_inc(s_vec, 1)
                mark_earlier(s + STEPS, q)
                dve.wait_ge(s_vec, s + 1)
                for g in range(2):
                    dve.wait_ge(s_rad, 2 * s + g + 1)
                    T = terms[:, g, :, :]
                    V.tensor_tensor(T[:, :, 0:256].rearrange("p k (o x) -> p k o x", o=16),
                                    ps[:, 4 + 2 * g:6 + 2 * g, 0:256].rearrange("p k (o x) -> p k o x", o=16),
                                    F[:, 2 * g:2 * g + 2, 0, :].unsqueeze(2).broadcast_to([P, 2, 16, 16]), ALU.mult)
                    for k in range(2):
                        ins = V.tensor_tensor(
                            T[:, k, 256:640].rearrange("p (u i x) -> p u i x", u=8, i=3),
                            ps[:, 4 + 2 * g + k, 256:384].rearrange("p (u x) -> p u x", u=8)
                            .unsqueeze(2).broadcast_to([P, 8, 3, 16]),
                            F[:, 2 * g + k, 1:4, :].unsqueeze(1).broadcast_to([P, 8, 3, 16]), ALU.mult)
                    ins.then_inc(s_terms, 1)
                if not first(s):
                    dve.wait_ge(s_prod[1], 4 * (s - 1))
                for g in range(2):
                    dve.wait_ge(s_terms, 2 * s + g + 1)
                    V.tensor_reduce(res[:, q, 2 * g:2 * g + 2, 0:40],
                                    terms[:, g, :, :].rearrange("p k (o x) -> p k o x", x=16), AX,
                                    ALU.add).then_inc(s_red, 1)
                entries(s + STEPS, q)
                dve.wait_ge(s_red, 2 * s + 2)
                V.tensor_tensor(along[:, :, :, :], res[:, q, :, 0:8].unsqueeze(3).broadcast_to([P, 4, 8, 3]),
                                r3[:, :, 0:3].unsqueeze(2).broadcast_to([P, 4, 8, 3]), ALU.mult).then_inc(s_along, 1)
                entry_places(s + STEPS)
                dve.wait_ge(s_along, s + 1)
                V.tensor_tensor(res[:, q, :, 16:40], res[:, q, :, 16:40],
                                along[:, :, :, :].rearrange("p k u i -> p k (u i)"), ALU.add).then_inc(s_msg, 1)
                dve.wait_ge(s_msg, s + 1)
                dve.wait_ge(s_wcol, s + 1)
                for k in range(4):
                    products(1, s, q, k, a_dst, res[:, q, k, 8:42], MSG)

            steps(dve, phase1)

            dve.wait_ge(s_idx, PAIRS)
            V.tensor_copy(late_idx[:, :], sc_idx[:, 2 * EARLY:2 * PAIRS])
            V.tensor_copy(late_val[:, :, :], sc_val[:, EARLY:PAIRS, 0, :]).then_inc(s_late, 1)

            dve.wait_ge(s_sum[1], CH)
            for part in range(PARTS[1]):
                rows = len(range(part, NA, PARTS[1]))
                acc = part_sums(1, part, MSG, rows).rearrange("p (a m) -> p a m", m=MSG)
                mine = slice(part, NA, PARTS[1])
                V.tensor_tensor(x[:, mine, :], x[:, mine, :], acc[:, :, 0:32], ALU.add)
                ins = V.tensor_copy(deg[:, mine, :], acc[:, :, 32:34])
            link(ins)
            layernorm()
            V.tensor_scalar(dinv[:, 0, :], deg[:, :, 0], 1.2e-35, None, ALU.max)
            V.tensor_scalar(dinv[:, 1, :], deg[:, :, 1], 1.0, None, ALU.add).then_inc(s_var, 1)
            std()
            link(V.reciprocal(dinv[:, :, :], dinv[:, :, :]))
            link(V.scalar_tensor_tensor(out=dinv[:, 0, :], in0=deg[:, :, 0], scalar=0.0, in1=dinv[:, 0, :],
                                        op0=ALU.is_gt, op1=ALU.mult))
            link(V.tensor_tensor(dinv[:, 1, :], dinv[:, 1, :], valid[:, :], ALU.mult))
            turned = ((0, 16, 7), (16, NA, 0))

            def part(a0, a1, bank):
                return ps[:, bank, 0:(a1 - a0) * FEAT].rearrange("p (a f) -> p a f", f=FEAT)

            def copy_sums(r):
                dve.wait_ge(s_mm, NA * (r + 1))
                for n in (0, 2, 4):
                    V.tensor_copy(aggT[:, n * 512:(n + 1) * 512], ps[:, n, :]).then_inc(s_aggc, 1)
                dve.wait_ge(s_turn, r + 1)

            V.tensor_tensor(zn[:, :, :], h[:, :, :], over_f(dinv[:, 0, :]), ALU.mult).then_inc(s_z, 1)
            link(V.tensor_scalar(cen[:, :, :], h[:, :, :], 1.0 - ALPHA, None, ALU.mult))
            for r in range(3):
                copy_sums(r)
                for a0, a1, bank in turned:
                    ins = V.tensor_tensor(sq[:, a0:a1, :], part(a0, a1, bank),
                                          dinv[:, 0, a0:a1].unsqueeze(2).broadcast_to([P, a1 - a0, FEAT]), ALU.mult)
                link(ins)
                link(V.scalar_tensor_tensor(out=h[:, :, :], in0=sq[:, :, :], scalar=ALPHA, in1=cen[:, :, :],
                                            op0=ALU.mult, op1=ALU.add))
                link(V.tensor_scalar(h[:, :, :], h[:, :, :], 0.0, 1.0, ALU.max, ALU.min))
                if r < 2:
                    V.tensor_tensor(zn[:, :, :], h[:, :, :], over_f(dinv[:, 0, :]), ALU.mult).then_inc(s_z, 1)
            link(V.tensor_tensor(x[:, :, :], x[:, :, :], h[:, :, :], ALU.add))
            layernorm()
            V.tensor_tensor(zn[:, :, :], h[:, :, :], over_f(dinv[:, 1, :]), ALU.mult).then_inc(s_z, 1)

            def over_nodes(i, r, src):
                V.tensor_reduce(fsum[:, 0, :], src.rearrange("p a f -> p f a"), AX, ALU.add).then_inc(s_fs, 1)
                dve.wait_ge(s_fsp, 2 * (r - 3) + i + 1)
                return ps[:, 1, i * FEAT:(i + 1) * FEAT]

            for r in range(3, 6):
                copy_sums(r)
                for a0, a1, bank in turned:
                    ins = V.tensor_tensor(sq[:, a0:a1, :], part(a0, a1, bank), zn[:, a0:a1, :], ALU.add)
                link(ins)
                link(V.scalar_tensor_tensor(out=h[:, :, :], in0=sq[:, :, :], scalar=0.0, in1=over_f(dinv[:, 1, :]),
                                            op0=ALU.max, op1=ALU.mult))
                link(V.tensor_scalar(fsum[:, 1, :], over_nodes(0, r, h[:, :, :]), 1.0 / NODES, None, ALU.mult))
                link(V.tensor_tensor(cen[:, :, :], h[:, :, :], over_a(fsum[:, 1, :]), ALU.subtract))
                link(V.tensor_scalar(cen[:, NA - 1, :], cen[:, NA - 1, :], valid[:, NA - 1:NA], None, ALU.mult))
                link(V.tensor_tensor(sq[:, :, :], cen[:, :, :], cen[:, :, :], ALU.mult))
                V.tensor_scalar(fsum[:, 2, :], over_nodes(1, r, sq[:, :, :]), 1.0 / NODES, EPS,
                                ALU.mult, ALU.add).then_inc(s_var, 1)
                std()
                link(V.reciprocal(fsum[:, 4, :], fsum[:, 3, :]))
                link(V.tensor_tensor(fsum[:, 4, :], fsum[:, 4, :], gam3[:, r - 3, :], ALU.mult))
                link(V.tensor_tensor(sq[:, :, :], cen[:, :, :], over_a(fsum[:, 4, :]), ALU.mult))
                link(V.tensor_tensor(h[:, :, :], sq[:, :, :], over_a(bet3[:, r - 3, :]), ALU.add))
                if r < 5:
                    V.tensor_tensor(zn[:, :, :], h[:, :, :], over_f(dinv[:, 1, :]), ALU.mult).then_inc(s_z, 1)
            V.tensor_tensor(x[:, :, :], x[:, :, :], h[:, :, :], ALU.add).then_inc(s_fin, 1)


_INS = [("x", (NP, FEAT)), ("src", (P, CH)), ("dst", (P, CH)), ("srcT", (112, 7 * P)), ("dstT", (112, 7 * P)),
        ("ea3", (P, CH * 3)), ("ea32", (P, CH * FEAT)), ("w", (P, CH)), ("wT", (CH, P)), ("w1T", (64, HID0)),
        ("b1", (HID0, 1)), ("gamma", (HID0, 1)), ("beta", (HID0, 1)), ("w2T", (HID0, FEAT)), ("b2", (1, FEAT)),
        ("l1w1", (HID1, 1)), ("l1b1", (HID1, 1)), ("l1w2", (HID1, 384)), ("l1b2", (1, 384)),
        ("gam3", (1, 3 * FEAT)), ("bet3", (1, 3 * FEAT))]


def kernel(**inputs):
    import numpy as _np
    import concourse.bacc as _bacc
    from concourse.bass_utils import run_bass_kernel_spmd as _run

    i = {k: _np.asarray(v) for k, v in inputs.items()}

    def padded(a, rows, fill):
        return _np.concatenate([a, _np.full((rows - a.shape[0],) + a.shape[1:], fill, a.dtype)])

    src, dst = (padded(i[k], CH * P, NP - 1).reshape(P, CH) for k in ("src", "dst"))
    w = padded(i["edge_weight"], CH * P, 0).reshape(P, CH)
    data = {
        "x": padded(i["x"], NP, 0), "src": src, "dst": dst,
        "srcT": src.T.reshape(112, 7 * P), "dstT": dst.T.reshape(112, 7 * P),
        "ea3": padded(i["edge_attr_3"], CH * P, 1).reshape(P, CH * 3),
        "ea32": padded(i["edge_attr_32"], CH * P, 0).reshape(P, CH * FEAT),
        "w": w, "wT": w.T,
        "w1T": i["L0_gnn_W1"].T, "b1": i["L0_gnn_b1"], "gamma": i["L0_gnn_gamma"], "beta": i["L0_gnn_beta"],
        "w2T": i["L0_gnn_W2"].T, "b2": i["L0_gnn_b2"],
        "l1w1": i["L1_gnn_w1"], "l1b1": i["L1_gnn_b1"], "l1w2": i["L1_gnn_w2"], "l1b2": i["L1_gnn_b2"],
        "gam3": i["L3_gnn_gammas"], "bet3": i["L3_gnn_betas"],
    }
    nc = _bacc.Bacc("TRN2", target_bir_lowering=False, num_devices=1)
    arrays, args = {}, []
    for name, shape in _INS:
        a = _np.ascontiguousarray(data[name].reshape(shape))
        arrays[f"in_{name}"] = a
        args.append(nc.dram_tensor(f"in_{name}", shape, mybir.dt.from_np(a.dtype), kind="ExternalInput").ap())
    args.append(nc.dram_tensor("out_0", (NODES, FEAT), F32, kind="ExternalOutput").ap())
    gnn_program(nc, *args)
    r = _run(nc, [arrays], core_ids=[0])
    return r.results[0]["out_0"]
```
